# Optimizing a Trainium2 kernel written in Bass

```python
import numpy as np
import jax
import jax.numpy as jnp

def _softmax(x, axis=-1):
    return jax.nn.softmax(x, axis=axis)

def _gelu(x):
    return jax.nn.gelu(x, approximate=True)

def _silu(x):
    return jax.nn.silu(x)

def _sigmoid(x):
    return jax.nn.sigmoid(x)

def _layernorm(x, axis=-1, eps=1e-05):
    m = jnp.mean(x, axis=axis, keepdims=True)
    v = jnp.var(x, axis=axis, keepdims=True)
    return (x - m) / jnp.sqrt(v + eps)

def _scatter_add(tgt, idx, src, axis=0):
    return tgt.at[idx].add(src)

def _segment_sum(src, seg, n):
    return jax.ops.segment_sum(src, seg, n)
kernel_name = 'mk_seq_postln_d2_jaxref_r8_3081af'

def setup_inputs(seed: int=0):
    np.random.seed(seed)
    _w = jnp.asarray

    def _L0_attn_setup():
        import jax, jax.numpy as jnp
        import numpy as np
        EMBED_DIM = 128
        NUM_HEADS = 16
        HEAD_DIM = EMBED_DIM // NUM_HEADS
        BATCH = 2
        SEQ = 256
        NEG_INF = float('-inf')
        key = jax.random.key(seed)
        k1, k2, k3, k4, k5 = jax.random.split(key, 5)
        return {'query': jax.random.normal(k1, (BATCH, SEQ, EMBED_DIM), dtype=jnp.float32), 'key': jax.random.normal(k2, (BATCH, SEQ, EMBED_DIM), dtype=jnp.float32), 'value': jax.random.normal(k3, (BATCH, SEQ, EMBED_DIM), dtype=jnp.float32), 'in_proj_weight': jax.random.normal(k4, (3 * EMBED_DIM, EMBED_DIM), dtype=jnp.float32) * (1.0 / np.sqrt(EMBED_DIM)), 'out_proj_weight': jax.random.normal(k5, (EMBED_DIM, EMBED_DIM), dtype=jnp.float32) * (1.0 / np.sqrt(EMBED_DIM))}
    _L0_attn_in = _L0_attn_setup()

    def _L0_ffn_setup():
        import jax, jax.numpy as jnp
        import numpy as np
        B, T, D, E = (4, 128, 128, 8)
        HD = 4 * D
        key = jax.random.key(seed)
        k1, k2, k3, k4 = jax.random.split(key, 4)
        std = 0.5 * D ** (-0.5)
        bound = 3.0 ** 0.5 * std
        x = jax.random.normal(k1, (B, T, D), dtype=jnp.float32)
        router_w = jax.random.normal(k2, (E, D), dtype=jnp.float32) * 0.02
        expert_fc = jax.random.uniform(k3, (E, D, HD), dtype=jnp.float32, minval=-bound, maxval=bound)
        expert_proj = jax.random.normal(k4, (E, D, HD), dtype=jnp.float32) * 0.02
        return {'x': x, 'router_w': router_w, 'expert_fc': expert_fc, 'expert_proj': expert_proj}
    _L0_ffn_in = _L0_ffn_setup()

    def _L1_attn_setup():
        import jax, jax.numpy as jnp
        import numpy as np
        WINDOW_SIZE = [4, 16, 64, 32]
        B, L, H = (8, 256, 128)
        D1 = 32
        key = jax.random.key(seed)
        ks = jax.random.split(key, 8)
        s = 0.02
        return {'query': jax.random.normal(ks[0], (B, L, H), jnp.float32), 'key_in': jax.random.normal(ks[1], (B, L, H), jnp.float32), 'value': jax.random.normal(ks[2], (B, L, H), jnp.float32), 'qkv_w': jax.random.normal(ks[3], (3 * H, H), jnp.float32) * s, 'qkv_b': jnp.zeros((3 * H,), jnp.float32), 'off_w': jax.random.normal(ks[4], (D1, H), jnp.float32) * s, 'lin2_w': jax.random.normal(ks[5], (1, D1), jnp.float32) * s, 'lin2_b': jnp.zeros((1,), jnp.float32)}
    _L1_attn_in = _L1_attn_setup()

    def _L1_ffn_setup():
        import jax, jax.numpy as jnp
        import numpy as np
        B, S, D = (4, 512, 128)
        DD = 4 * D
        N_EXPERTS = 8
        CAPACITY = 1.0
        LN_EPS = 1e-05
        key = jax.random.key(seed)
        ks = jax.random.split(key, 8)
        s1 = 1.0 / np.sqrt(D)
        s2 = 1.0 / np.sqrt(DD)
        return {'x': jax.random.normal(ks[0], (B, S, D), jnp.float32), 'gate_w': jax.random.normal(ks[1], (N_EXPERTS, D), jnp.float32) * 0.02, 'ln_w': jnp.ones((D,), jnp.float32), 'ln_b': jnp.zeros((D,), jnp.float32), 'fc1s': jax.random.normal(ks[2], (N_EXPERTS, DD, D), jnp.float32) * s1, 'b1s': jax.random.normal(ks[3], (N_EXPERTS, DD), jnp.float32) * s1, 'fc2s': jax.random.normal(ks[4], (N_EXPERTS, D, DD), jnp.float32) * s2, 'b2s': jax.random.normal(ks[5], (N_EXPERTS, D), jnp.float32) * s2}
    _L1_ffn_in = _L1_ffn_setup()
    _d = {'L0_attn_query': _L0_attn_in['query'], 'L0_attn_key': _L0_attn_in['key'], 'L0_attn_value': _L0_attn_in['value'], 'L0_attn_in_proj_weight': _L0_attn_in['in_proj_weight'], 'L0_attn_out_proj_weight': _L0_attn_in['out_proj_weight'], 'L0_ffn_router_w': _L0_ffn_in['router_w'], 'L0_ffn_expert_fc': _L0_ffn_in['expert_fc'], 'L0_ffn_expert_proj': _L0_ffn_in['expert_proj'], 'L1_attn_key_in': _L1_attn_in['key_in'], 'L1_attn_value': _L1_attn_in['value'], 'L1_attn_qkv_w': _L1_attn_in['qkv_w'], 'L1_attn_qkv_b': _L1_attn_in['qkv_b'], 'L1_attn_off_w': _L1_attn_in['off_w'], 'L1_attn_lin2_w': _L1_attn_in['lin2_w'], 'L1_attn_lin2_b': _L1_attn_in['lin2_b'], 'L1_ffn_gate_w': _L1_ffn_in['gate_w'], 'L1_ffn_ln_w': _L1_ffn_in['ln_w'], 'L1_ffn_ln_b': _L1_ffn_in['ln_b'], 'L1_ffn_fc1s': _L1_ffn_in['fc1s'], 'L1_ffn_b1s': _L1_ffn_in['b1s'], 'L1_ffn_fc2s': _L1_ffn_in['fc2s'], 'L1_ffn_b2s': _L1_ffn_in['b2s']}
    _x0 = _d['L0_attn_query']
    _d['L0_attn_query'] = jax.random.normal(jax.random.fold_in(jax.random.key(seed), 1), (16, 256, 128), dtype=_x0.dtype)
    del _x0
    return _d

def reference(L0_attn_query, L0_attn_key, L0_attn_value, L0_attn_in_proj_weight, L0_attn_out_proj_weight, L0_ffn_router_w, L0_ffn_expert_fc, L0_ffn_expert_proj, L1_attn_key_in, L1_attn_value, L1_attn_qkv_w, L1_attn_qkv_b, L1_attn_off_w, L1_attn_lin2_w, L1_attn_lin2_b, L1_ffn_gate_w, L1_ffn_ln_w, L1_ffn_ln_b, L1_ffn_fc1s, L1_ffn_b1s, L1_ffn_fc2s, L1_ffn_b2s):

    def _L0_attn_ref(query, key, value, in_proj_weight, out_proj_weight):
        import jax, jax.numpy as jnp
        import numpy as np
        EMBED_DIM = 128
        NUM_HEADS = 16
        HEAD_DIM = EMBED_DIM // NUM_HEADS
        BATCH = 2
        SEQ = 256
        NEG_INF = float('-inf')
        B, T, E = query.shape
        H, D = (NUM_HEADS, HEAD_DIM)
        projected = jnp.einsum('bte,fe->btf', query, in_proj_weight)
        packed = projected.reshape(B, T, 3, H, D).transpose(0, 3, 2, 1, 4)
        q, k, v = (packed[:, :, 0], packed[:, :, 1], packed[:, :, 2])
        q = q / jnp.sqrt(jnp.asarray(D, dtype=q.dtype))
        attention = jnp.einsum('bhtd,bhkd->bhtk', q, k)
        qpos = jnp.arange(T)[:, None]
        kpos = jnp.arange(T)[None, :]
        mask = jnp.where(qpos - kpos >= 0, 0.0, NEG_INF).astype(attention.dtype)
        attention = attention + mask[None, None]
        activation = jax.nn.softmax(attention, axis=-1)
        x = jnp.einsum('bhtk,bhkd->bhtd', activation, v)
        x = x.transpose(0, 2, 1, 3).reshape(B, T, E)
        out = jnp.einsum('bte,fe->btf', x, out_proj_weight)
        return out

    def _L0_ffn_ref(x, router_w, expert_fc, expert_proj):
        import jax, jax.numpy as jnp
        import numpy as np
        B, T, D, E = (4, 128, 128, 8)
        HD = 4 * D
        logits = jnp.einsum('btd,ed->bte', x, router_w)
        probs = jax.nn.softmax(logits, axis=-1)
        expert_ids = jnp.argmax(probs, axis=-1)
        mask = jax.nn.one_hot(expert_ids, E, dtype=x.dtype)
        h = jnp.einsum('btd,edh->ebth', x, expert_fc)
        h = jnp.square(jax.nn.relu(h))
        out_e = jnp.einsum('ebth,edh->ebtd', h, expert_proj)
        output = jnp.einsum('ebtd,bte->btd', out_e, mask)
        return output

    def _L1_attn_ref(query, key_in, value, qkv_w, qkv_b, off_w, lin2_w, lin2_b):
        import jax, jax.numpy as jnp
        import numpy as np
        WINDOW_SIZE = [4, 16, 64, 32]
        B, L, H = (8, 256, 128)
        D1 = 32
        Bq, Lq, Hq = query.shape
        G = len(WINDOW_SIZE)
        d = Hq // G
        qkv = (query @ qkv_w.T + qkv_b).reshape(Bq, Lq, 3, Hq).transpose(2, 0, 1, 3)
        idx = jnp.arange(Lq)
        absdiff = jnp.abs(idx[:, None] - idx[None, :]).astype(jnp.float32)
        win_mask = jnp.where(idx[None, :] < idx[:, None], 1e+18, absdiff)
        dx_base = jax.nn.sigmoid(jax.nn.relu(query) @ off_w.T @ lin2_w.T + lin2_b) * Lq
        scale = 1.0 / np.sqrt(Lq)
        outs = []
        for i, ws in enumerate(WINDOW_SIZE):
            q = qkv[0, :, :, i * d:(i + 1) * d]
            k = qkv[1, :, :, i * d:(i + 1) * d]
            v = qkv[2, :, :, i * d:(i + 1) * d]
            dx = dx_base + ws
            scores = jnp.einsum('bld,bmd->blm', q, k) * scale
            scores = jnp.where(win_mask[None, :, :] > dx, -1e+18, scores) + scores
            attn = jax.nn.softmax(scores, axis=-1)
            outs.append(jnp.einsum('blm,bmd->bld', attn, v))
        return jnp.concatenate(outs, axis=-1)

    def _L1_ffn_ref(x, gate_w, ln_w, ln_b, fc1s, b1s, fc2s, b2s):
        import jax, jax.numpy as jnp
        import numpy as np
        B, S, D = (4, 512, 128)
        DD = 4 * D
        N_EXPERTS = 8
        CAPACITY = 1.0
        LN_EPS = 1e-05
        og_shape = x.shape
        d = og_shape[-1]
        xf = x.reshape(-1, d)
        bs = xf.shape[0]
        n = gate_w.shape[0]
        k = int(bs * CAPACITY) // n
        scores = jax.nn.softmax(xf @ gate_w.T, axis=-1)
        vals, idx = jax.lax.top_k(scores.T, k)
        kept_w = vals.T
        kept_idx = idx.T
        flat_idx = kept_idx.reshape(-1)
        y = xf[flat_idx].reshape(k, n, d)
        mu = y.mean(-1, keepdims=True)
        var = ((y - mu) ** 2).mean(-1, keepdims=True)
        y = (y - mu) * jax.lax.rsqrt(var + LN_EPS) * ln_w + ln_b
        h = jnp.einsum('knd,nfd->knf', y, fc1s) + b1s
        h = jax.nn.gelu(h, approximate=True)
        out = jnp.einsum('knf,ndf->knd', h, fc2s) + b2s
        out = out * kept_w[..., None]
        xf = xf.at[flat_idx].add(out.reshape(k * n, d))
        return xf.reshape(og_shape)
    x = L0_attn_query
    x = _layernorm(x + _L0_attn_ref(x, L0_attn_key, L0_attn_value, L0_attn_in_proj_weight, L0_attn_out_proj_weight), axis=-1)
    x = _layernorm(x + _L0_ffn_ref(x, L0_ffn_router_w, L0_ffn_expert_fc, L0_ffn_expert_proj), axis=-1)
    x = _layernorm(x + _L1_attn_ref(x, L1_attn_key_in, L1_attn_value, L1_attn_qkv_w, L1_attn_qkv_b, L1_attn_off_w, L1_attn_lin2_w, L1_attn_lin2_b), axis=-1)
    x = _layernorm(x + _L1_ffn_ref(x, L1_ffn_gate_w, L1_ffn_ln_w, L1_ffn_ln_b, L1_ffn_fc1s, L1_ffn_b1s, L1_ffn_fc2s, L1_ffn_b2s), axis=-1)
    return x

_drawn_inputs = setup_inputs


def setup_inputs(seed=0):
    import zlib

    import numpy as np

    out = dict(_drawn_inputs(seed))
    spreads = {'L1_attn_qkv_b': (0.0, 0.1), 'L1_ffn_ln_w': (1.0, 0.6), 'L1_ffn_ln_b': (0.0, 0.8)}
    factors = {'L1_attn_off_w': 50.976, 'L1_attn_lin2_w': 47.483, 'L1_ffn_b1s': 8.0, 'L1_ffn_b2s': 8.0}
    for name, (base, spread) in spreads.items():
        noise = np.random.default_rng([zlib.crc32(name.encode()), seed]).standard_normal(out[name].shape)
        drawn = base * np.exp(spread * noise) if base else spread * noise
        out[name] = jnp.asarray(drawn.astype(out[name].dtype))
    for name, factor in factors.items():
        out[name] = (out[name] * factor).astype(out[name].dtype)
    return out
```

```python
import concourse.bass as bass
from concourse import mybir
from contextlib import ExitStack

f32 = mybir.dt.float32
bf16 = mybir.dt.bfloat16
i32 = mybir.dt.int32
ALU = mybir.AluOpType
ACT = mybir.ActivationFunctionType
AX = mybir.AxisListType

D = 128
T = 256
NTOK = 4096
NB = NTOK // T
NT = NTOK // 128
H0 = 16
DH0 = D // H0
BIG = 1e30
EPS = 1e-5


class Seq:

    def __init__(self, j, k):
        self.n = 2 * j + k
        self.half = j + k // 2
        self.p = k % 2


class Quad:

    def __init__(self, j, k):
        self.n = 4 * j + k
        self.four = j + k // 4
        self.q, self.p = k % 4, k % 2


def later(s, n=2):
    return not (isinstance(s.n, int) and s.n < n)


class Steps:

    def __init__(self, eng, sem, seq, total):
        self.eng, self.sem, self.base, self.total, self.done = eng, sem, seq.n * total, total, 0

    def __call__(self, ins):
        self.done += 1
        assert self.done <= self.total
        ins.then_inc(self.sem, 1)
        self.eng.wait_ge(self.sem, self.base + self.done)


def hold(A, eng):
    eng.sem_inc(A["held"], 1)


def attention0(nc, A, x, x1d, qkd, wqkvT, woT, routerT, logits, NB=NB):
    ctx = ExitStack()
    with ctx:
        def sb(name, shape, dt=f32):
            return ctx.enter_context(nc.sbuf_tensor("a0_" + name, shape, dt))

        used = []

        def sem(name):
            used.append(ctx.enter_context(nc.semaphore("a0_" + name)))
            return used[-1]

        ident, identb = A["ident"], A["identb"]
        wq = sb("wq", [D, 3 * D])
        wo = sb("wo", [D, D])
        wr = sb("wr", [D, 8])
        maskA = sb("maskA", [128, 4, 128], bf16)
        maskB = sb("maskB", [128, 2, 128], bf16)
        zrows = sb("zrows", [2, 8 * T], bf16)
        xp = [sb(f"xp{p}", [128, 2, D]) for p in range(2)]
        xr = [sb(f"xr{p}", [128, 2, D]) for p in range(2)]
        xT = [sb(f"xT{p}", [D, T]) for p in range(2)]
        hml = [sb(f"hml{p}", [128, 2, 3, T], bf16) for p in range(2)]
        rest = sb("rest", [128, 2, T])
        va = [sb(f"va{p}", [128, 2, H0, 32]) for p in range(2)]
        qs = [sb(f"qs{p}", [128, H0, T], bf16) for p in range(2)]
        ks = [sb(f"ks{p}", [128, H0, T], bf16) for p in range(2)]
        mx = [sb(f"mx{p}", [128, H0, 2]) for p in range(2)]
        ms = [sb(f"ms{p}", [128, 2, H0, 2], bf16) for p in range(2)]
        mrow = [sb(f"mrow{p}", [64, 128], bf16) for p in range(2)]
        pr = [sb(f"pr{p}", [128, 3 * T]) for p in range(2)]
        oT = [sb(f"oT{p}", [128, T]) for p in range(2)]
        rc = sb("rc", [128, 2, 4])
        on = [sb(f"on{p}", [128, 2, D]) for p in range(2)]
        onT = sb("onT", [D, T])
        y = sb("y", [128, 2, D])
        st = sb("st", [128, 2, 6])
        mv = sb("mv", [128, 2, 2])
        vareps, rstd = sb("vareps", [128, 2, 1]), sb("rstd", [128, 2, 1])
        x1 = [sb(f"x1_{p}", [128, 2, D]) for p in range(2)]
        x1T = sb("x1T", [D, T])
        mhalf = A["mhalf"]

        psB = [ctx.enter_context(nc.psum_tensor(f"a0_psB{p}", [128, 1024], f32)) for p in range(2)]
        psA = [ctx.enter_context(nc.psum_tensor(f"a0_psA{p}", [128, 512], f32)) for p in range(2)]
        psO = ctx.enter_context(nc.psum_tensor("a0_psO", [128, 512], f32))
        psM = ctx.enter_context(nc.psum_tensor("a0_psM", [128, 512], f32))

        w_in, filled, consts, wq_scaled = sem("w_in"), sem("filled"), sem("consts"), sem("wq_scaled")
        xp_in = [sem(f"xp_in{p}") for p in range(2)]
        xr_in = [sem(f"xr_in{p}") for p in range(2)]
        stack_in = [[sem(f"stack_in{p}{g}") for g in range(2)] for p in range(2)]
        rows_in = [sem(f"rows_in{p}") for p in range(2)]
        hml_out = [sem(f"hml_out{p}") for p in range(2)]
        x1_out = [sem(f"x1_out{p}") for p in range(2)]
        xT_ps, xT_sb = sem("xT_ps"), sem("xT_sb")
        qk_ps, qk_high, qk_rest, qk_mid, qk_low = (sem(n) for n in ("qk_ps", "qk_high", "qk_rest", "qk_mid", "qk_low"))
        v_ps, v_sb = sem("v_ps"), sem("v_sb")
        a_ps, a_max = sem("a_ps"), sem("a_max")
        split_step = sem("split_step")
        mT_ps, mT_sb = sem("mT_ps"), sem("mT_sb")
        s_ps, probs, pv_done = sem("s_ps"), sem("probs"), sem("pv_done")
        o_sb, otr_ps, on_step, on_sb = sem("o_sb"), sem("otr_ps"), sem("on_step"), sem("on_sb")
        onT_ps, onT_sb, y_ps, ln_step, var_sb, rstd_sb, x1_sb = (sem(n) for n in ("onT_ps", "onT_sb", "y_ps", "ln_step", "var_sb", "rstd_sb", "x1_sb"))
        y_sb = sem("y_sb")
        x1T_ps, x1T_sb, lg_ps, lg_sb = (sem(n) for n in ("x1T_ps", "x1T_sb", "lg_ps", "lg_sb"))

        work = ExitStack()
        block = work.enter_context(nc.Block())

        def iterations(eng, body):
            def peeled(i):
                def seq(off):
                    return Seq(0, i + off) if 0 <= i + off < NB else None
                body(seq(-1), seq(0), seq(1), seq(2))
            for i in range(-2, 2):
                peeled(i)
            full = (NB - 2 - 2) // 2
            with eng.Fori(1, 1 + full) as j:
                for k in range(2):
                    body(Seq(j, k - 1) if k else Seq(j - 1, 1), Seq(j, k), Seq(j, k + 1), Seq(j, k + 2))
            for i in range(NB - 2, NB + 1):
                peeled(i)

        @block.sync
        def _(sp):
            sp.dma_start(wq[:], wqkvT).then_inc(w_in, 16)
            sp.dma_start(wo[:], woT).then_inc(w_in, 16)
            sp.dma_start(wr[:], routerT).then_inc(w_in, 16)
            xv = x.rearrange("(b t p) d -> b p t d", t=2, p=128)
            x1v = x1d.rearrange("(b t p) d -> b p t d", t=2, p=128)

            def load_xp(s):
                sp.dma_start(xp[s.p][:], xv[s.n]).then_inc(xp_in[s.p], 16)

            def load_stacks(s, g):
                heads = slice(8 * g, 8 * g + 8)
                row = 0
                for n in (3, 2, 1):
                    for dst, c, r0 in ((qs, 0, 0), (ks, 1, 3 - n)):
                        src = qkd[s.p][c, r0:r0 + n].rearrange("r (d h) t -> (r d) h t", h=H0)
                        sp.dma_start(dst[s.p][row:row + 8 * n, heads, :], src[:, heads, :]
                                     ).then_inc(stack_in[s.p][g], 16)
                    row += 8 * n
                sp.dma_start(qs[s.p][64:66, heads, :], zrows[:].rearrange("r (h t) -> r h t", h=8)
                             ).then_inc(stack_in[s.p][g], 16)

            def body(F, B, Am, P):
                if P:
                    if F or B:
                        sp.wait_ge(xT_ps, P.n - 1)
                    load_xp(P)
                if F:
                    if not (isinstance(F.n, int) and F.n < 2):
                        sp.wait_ge(y_sb, F.n - 1)
                    sp.dma_start(xr[F.p][:], xv[F.n]).then_inc(xr_in[F.p], 16)
                if Am:
                    if F:
                        sp.wait_ge(s_ps, 8 * F.n + 8)
                    load_stacks(Am, 1)
                if P:
                    sp.wait_ge(qk_high, P.n + 1)
                    sp.wait_ge(qk_low, P.n + 1)
                    sp.dma_start(qkd[P.p].rearrange("c r f t -> f c r t"), hml[P.p][:]).then_inc(hml_out[P.p], 16)
                    sp.wait_ge(hml_out[P.p], 16 * (P.half + 1))
                    if B:
                        sp.wait_ge(s_ps, 8 * B.n + 4)
                    load_stacks(P, 0)
                if F:
                    sp.wait_ge(x1_sb, F.n + 1)
                    sp.dma_start(x1v[F.n], x1[F.p][:]).then_inc(x1_out[F.p], 16)
                if Am:
                    sp.wait_ge(mT_sb, Am.n + 1)
                    sp.dma_start(qs[Am.p][64:66, :, :], mrow[Am.p][:]).then_inc(rows_in[Am.p], 16)
            sp.wait_ge(consts, 1)
            iterations(sp, body)
            for p in range(2):
                sp.wait_ge(x1_out[p], 16 * (NB // 2))

        def unit(n):
            g, m = n // 3, n % 3
            return (0, range(4 * g, 4 * g + 4)) if m == 0 else (1, range(4 * g + 2 * (m - 1), 4 * g + 2 * m))

        @block.tensor
        def _(pe):
            mm = nc.tensor.matmul
            pe.wait_ge(w_in, 48)
            pe.wait_ge(consts, 1)
            pe.wait_ge(wq_scaled, 1)

            def scores_for_max(s, n):
                t, heads = unit(n)
                if n % 3 == 0 and n // 3 in (0, 2):
                    pe.wait_ge(stack_in[s.p][n // 6], 16 * 7 * (s.half + 1))
                if not (isinstance(s.n, int) and 12 * s.n + n < 2):
                    pe.wait_ge(a_max, 12 * s.n + n - 1)
                bank = psA[n % 2]
                w = 128 if t == 0 else T
                out = bank[:].rearrange("p (h k) -> p h k", k=w)
                if t == 0:
                    mm(bank[:], identb[:], maskA[:], start=True, stop=True)
                else:
                    mm(out[:, :, 128:256], identb[:], maskA[:, 0:2, :], start=True, stop=True)
                for i, h in enumerate(heads):
                    last = mm(out[:, i, :], qs[s.p][:, h, 128 * t:128 * t + 128], ks[s.p][:, h, 0:w],
                              start=False, stop=True, skip_group_check=True)
                last.then_inc(a_ps, 1)

            def scores(s, u):
                if u == 0:
                    pe.wait_ge(rows_in[s.p], 16 * (s.half + 1))
                if not (isinstance(s.n, int) and 8 * s.n + u < 2):
                    pe.wait_ge(probs, 8 * s.n + u - 1)
                b = psB[u % 2]
                k0 = b[:, 0:512].rearrange("p (h q) -> p h q", q=T)
                k1 = b[:, 512:768].rearrange("p (h q) -> p h q", q=128)
                mm(k0[:, :, 0:128], identb[:], maskB[:], start=True, stop=True)
                for i in range(2):
                    mm(k0[:, i, :], ks[s.p][:, 2 * u + i, 0:128], qs[s.p][:, 2 * u + i, :], start=False,
                       stop=True, skip_group_check=True)
                mm(k1, identb[:], maskB[:], start=True, stop=True)
                for i in range(2):
                    last = mm(k1[:, i, :], ks[s.p][:, 2 * u + i, 128:256], qs[s.p][:, 2 * u + i, 128:256],
                              start=False, stop=True, skip_group_check=True)
                last.then_inc(s_ps, 1)

            def weigh_values(s, u):
                pe.wait_ge(probs, 8 * s.n + u + 1)
                if u == 0:
                    pe.wait_ge(v_sb, s.n + 1)
                if u % 2 == 0 and not (isinstance(s.n, int) and 4 * s.n + u // 2 < 1):
                    pe.wait_ge(o_sb, 4 * s.n + u // 2)
                p0 = pr[u % 2][:, 0:512].rearrange("p (h q) -> p h q", q=T)
                p1 = pr[u % 2][:, 512:768].rearrange("p (h q) -> p h q", q=128)
                for i in range(2):
                    c = 2 * (u % 2) + i
                    q = slice(32 * c, 32 * c + 32)
                    mm(psO[q, 0:T], va[s.p][:, 0, 2 * u + i, :], p0[:, i, :], start=True, stop=True,
                       tile_position=(0, 32 * c))
                for i in range(2):
                    c = 2 * (u % 2) + i
                    q = slice(32 * c, 32 * c + 32)
                    last = mm(psO[q, 128:T], va[s.p][:, 1, 2 * u + i, :], p1[:, i, :], start=False, stop=True,
                              tile_position=(0, 32 * c), skip_group_check=True)
                last.then_inc(pv_done, 1)

            def tr(out, in_):
                return nc.tensor.transpose(out, in_, ident[:])

            def x_transpose(s):
                pe.wait_ge(xp_in[s.p], 16 * (s.half + 1))
                for t in range(2):
                    last = tr(psM[:, 128 * t:128 * t + 128], xp[s.p][:, t, :])
                last.then_inc(xT_ps, 1)

            def project_qk(s):
                pe.wait_ge(xT_sb, s.n + 1)
                for c in range(2):
                    last = mm(psM[:, T * c:T * c + T], wq[:, D * c:D * c + D], xT[s.p][:], start=True, stop=True)
                last.then_inc(qk_ps, 1)

            def project_v(s):
                for t in range(2):
                    last = mm(psM[:, D * t:D * t + D], xT[s.p][:, 128 * t:128 * t + 128], wq[:, 2 * D:3 * D],
                              start=True, stop=True)
                last.then_inc(v_ps, 1)

            def o_transpose(s, g):
                pe.wait_ge(o_sb, 4 * s.n + g + 1)
                for t in range(2):
                    last = tr(psM[:, 128 * t:128 * t + 128], oT[g % 2][:, 128 * t:128 * t + 128])
                last.then_inc(otr_ps, 1)

            def on_transpose(s):
                pe.wait_ge(on_sb, 4 * s.n + 4)
                for t in range(2):
                    last = tr(psM[:, 128 * t:128 * t + 128], on[s.p][:, t, :])
                last.then_inc(onT_ps, 1)

            def out_project(s):
                pe.wait_ge(onT_sb, s.n + 1)
                for t in range(2):
                    last = mm(psM[:, D * t:D * t + D], onT[:, 128 * t:128 * t + 128], wo[:], start=True, stop=True)
                last.then_inc(y_ps, 1)

            def x1_transpose(s):
                pe.wait_ge(x1_sb, s.n + 1)
                for t in range(2):
                    last = tr(psM[:, 128 * t:128 * t + 128], x1[s.p][:, t, :])
                last.then_inc(x1T_ps, 1)

            def route(s):
                pe.wait_ge(x1T_sb, s.n + 1)
                for t in range(2):
                    last = mm(psM[:, 8 * t:8 * t + 8], x1T[:, 128 * t:128 * t + 128], wr[:], start=True, stop=True)
                last.then_inc(lg_ps, 1)

            def max_rows(s):
                pe.wait_ge(split_step, 2 * s.n + 2)
                hold(A, pe)
                nc.tensor.transpose(psM[0:64, 0:64].bitcast(bf16), ms[s.p][:].rearrange("p a h t -> p (a h t)"),
                                    identb[:]).then_inc(mT_ps, 1)

            def body(F, B, Am, P):
                left = [None]

                def psm_step(f, s, *a, freed):
                    if s is None:
                        return
                    if left[0]:
                        pe.wait_ge(*left[0])
                    f(s, *a)
                    left[0] = freed

                psm_first(pe, F, B, Am, P)
                for u in range(8):
                    if Am and u < 6:
                        scores_for_max(Am, 2 * u)
                        scores_for_max(Am, 2 * u + 1)
                    if B:
                        scores(B, u)
                    if u == 0:
                        psm_step(x_transpose, P, freed=P and (xT_sb, P.n + 1))
                        if F:
                            weigh_values(F, 7)
                    elif B:
                        weigh_values(B, u - 1)
                    if u == 1:
                        psm_step(o_transpose, F, 3, freed=F and (on_sb, 4 * F.n + 4))
                        psm_step(project_qk, P, freed=P and (qk_rest, P.n + 1))
                    if u == 2:
                        if P:
                            pe.wait_ge(qk_high, P.n + 1)
                        psm_step(on_transpose, F, freed=F and (onT_sb, F.n + 1))
                        psm_step(project_v, Am, freed=Am and (v_sb, Am.n + 1))
                    if u == 3:
                        psm_step(o_transpose, B, 0, freed=B and (on_sb, 4 * B.n + 1))
                        psm_step(out_project, F, freed=F and (y_sb, F.n + 1))
                    if u == 4:
                        psm_step(x1_transpose, F, freed=F and (x1T_sb, F.n + 1))
                    if u == 5:
                        psm_step(o_transpose, B, 1, freed=B and (on_sb, 4 * B.n + 2))
                        psm_step(route, F, freed=F and (lg_sb, F.n + 1))
                    if u == 6:
                        psm_step(max_rows, Am, freed=Am and (mT_sb, Am.n + 1))
                    if u == 7:
                        psm_step(o_transpose, B, 2, freed=B and (on_sb, 4 * B.n + 3))

            def psm_first(pe, F, B, Am, P):
                if F:
                    pe.wait_ge(on_sb, 4 * F.n + 3)
                elif B:
                    pe.wait_ge(mT_sb, B.n + 1)
                elif Am:
                    pe.wait_ge(qk_rest, Am.n + 1)

            iterations(pe, body)

        @block.scalar
        def _(act):
            cp = nc.scalar.copy
            act.wait_ge(w_in, 48)
            nc.scalar.mul(wq[:, 0:D], wq[:, 0:D], DH0 ** -0.5).then_inc(wq_scaled, 1)

            def body(F, B, Am, P):
                for u in range(8):
                    if u == 0 and P:
                        act.wait_ge(xT_ps, P.n + 1)
                        cp(xT[P.p][:], psM[:, 0:T]).then_inc(xT_sb, 1)
                    if u == 1 and F:
                        act.wait_ge(pv_done, 8 * F.n + 8)
                        cp(oT[1][:], psO[:, 0:T]).then_inc(o_sb, 1)
                    if B:
                        act.wait_ge(s_ps, 8 * B.n + u + 1)
                        if not (isinstance(B.n, int) and 8 * B.n + u < 2):
                            act.wait_ge(pv_done, 8 * B.n + u - 1)
                        nc.scalar.activation(pr[u % 2][:], psB[u % 2][:, 0:3 * T], ACT.Exp).then_inc(probs, 1)
                    if u == 1 and P:
                        act.wait_ge(qk_ps, P.n + 1)
                        if not (isinstance(P.n, int) and P.n < 2):
                            act.wait_ge(hml_out[P.p], 16 * P.half)
                        for c, r in ((0, 0), (1, 2)):
                            ins = cp(hml[P.p][:, c, r, :], psM[:, T * c:T * c + T])
                        ins.then_inc(qk_high, 1)
                    if u == 2:
                        if F:
                            act.wait_ge(onT_ps, F.n + 1)
                            cp(onT[:], psM[:, 0:T]).then_inc(onT_sb, 1)
                        if Am:
                            act.wait_ge(v_ps, Am.n + 1)
                            if F:
                                act.wait_ge(pv_done, 8 * Am.n - 8)
                            cp(va[Am.p][:, :, :, 0:DH0], psM[:, 0:T].rearrange("p (t h d) -> p t h d", t=2, d=DH0)
                               ).then_inc(v_sb, 1)
                    if u in (2, 4, 6) and B:
                        g = u // 2 - 1
                        act.wait_ge(pv_done, 8 * B.n + 2 * g + 2)
                        if not (isinstance(B.n, int) and 4 * B.n + g < 2):
                            act.wait_ge(otr_ps, 4 * B.n + g - 1)
                        cp(oT[g % 2][:], psO[:, 0:T]).then_inc(o_sb, 1)
                    if u == 4 and F:
                        act.wait_ge(x1T_ps, F.n + 1)
                        cp(x1T[:], psM[:, 0:T]).then_inc(x1T_sb, 1)
            iterations(act, body)

        @block.gpsimd
        def _(pool):
            g = nc.gpsimd
            g.memset(maskA[:], 0.0)
            g.memset(maskB[:], 0.0)
            g.memset(zrows[:], 0.0)
            for p in range(2):
                g.memset(va[p][:], 1.0)
                g.memset(qs[p][:], 0.0)
                g.memset(ks[p][:], 0.0).then_inc(filled, 1)
            pool.wait_ge(filled, 2)
            for p in range(2):
                last = g.memset(ks[p][64:66, :, :], -1.0)
            last.then_inc(filled, 1)
            pool.wait_ge(filled, 3)
            g.affine_select(out=maskA[:], in_=maskA[:], pattern=[[0, 4], [-1, 128]], compare_op=ALU.is_ge,
                            fill=-BIG, base=0, channel_multiplier=1)
            g.affine_select(out=maskB[:], in_=maskB[:], pattern=[[0, 2], [1, 128]], compare_op=ALU.is_ge,
                            fill=-BIG, base=0, channel_multiplier=-1).then_inc(consts, 1)

            def body(F, B, Am, P):
                if P:
                    pool.wait_ge(qk_rest, P.n + 1)
                    hold(A, pool)
                    g.tensor_copy(hml[P.p][:, :, 1, :], rest[:]).then_inc(qk_mid, 1)
                    pool.wait_ge(qk_mid, P.n + 1)
                    g.tensor_tensor(hml[P.p][:, 0, 2, :], rest[:, 0, :], hml[P.p][:, 0, 1, :], ALU.subtract)
                    g.tensor_tensor(hml[P.p][:, 1, 0, :], rest[:, 1, :], hml[P.p][:, 1, 1, :], ALU.subtract
                                    ).then_inc(qk_low, 1)
                if F:
                    pool.wait_ge(var_sb, F.n + 1)
                    g.tensor_tensor(rstd[:], vareps[:], mhalf[:, 0:2], ALU.pow).then_inc(rstd_sb, 1)
            iterations(pool, body)

        @block.vector
        def _(dve):
            v = nc.vector

            def maxima(s, n):
                t, heads = unit(n)
                dve.wait_ge(a_ps, 12 * s.n + n + 1)
                if n == 0 and not (isinstance(s.n, int) and s.n < 2):
                    dve.wait_ge(split_step, 2 * s.n - 2)
                v.tensor_reduce(mx[s.p][:, heads[0]:heads[0] + len(heads), t],
                                psA[n % 2][:].rearrange("p (h k) -> p h k", h=len(heads)), AX.X, ALU.max
                                ).then_inc(a_max, 1)

            def normalise(s, g):
                dve.wait_ge(otr_ps, 4 * s.n + g + 1)
                o = psM[:, 0:T].rearrange("p (t j r) -> p t j r", t=2, r=32)
                v.reciprocal(rc[:], o[:, :, :, DH0]).then_inc(on_step, 1)
                dve.wait_ge(on_step, 4 * s.n + g + 1)
                if g == 0 and not (isinstance(s.n, int) and s.n < 2):
                    dve.wait_ge(onT_ps, s.n - 1)
                v.tensor_tensor(on[s.p][:, :, 32 * g:32 * g + 32].rearrange("p t (j d) -> p t j d", d=DH0),
                                o[:, :, :, 0:DH0], rc[:].unsqueeze(3).broadcast_to([128, 2, 4, DH0]), ALU.mult).then_inc(on_sb, 1)

            def body(F, B, Am, P):
                for u in range(8):
                    if Am and u < 6:
                        maxima(Am, 2 * u)
                    if u == 4 and F:
                        scale_x1(F)
                    if Am and u < 6:
                        maxima(Am, 2 * u + 1)
                    if u == 1:
                        if F:
                            normalise(F, 3)
                        if P:
                            dve.wait_ge(qk_high, P.n + 1)
                            if not (isinstance(P.n, int) and P.n < 1):
                                dve.wait_ge(qk_low, P.n)
                            v.tensor_tensor(rest[:, 0, :], psM[:, 0:T], hml[P.p][:, 0, 0, :], ALU.subtract)
                            v.tensor_tensor(rest[:, 1, :], psM[:, T:2 * T], hml[P.p][:, 1, 2, :], ALU.subtract
                                            ).then_inc(qk_rest, 1)
                    if u == 3:
                        if B:
                            normalise(B, 0)
                        if F:
                            dve.wait_ge(y_ps, F.n + 1)
                            dve.wait_ge(xr_in[F.p], 16 * (F.half + 1))
                            layer_norm(F)
                    if u == 5:
                        if B:
                            normalise(B, 1)
                        if F:
                            dve.wait_ge(lg_ps, F.n + 1)
                            v.tensor_copy(logits[:, bass.ds(2 * F.n, 2), :] ,
                                          psM[:, 0:16].rearrange("p (t e) -> p t e", e=8)).then_inc(lg_sb, 1)
                    if u == 6 and Am:
                        step = Steps(dve, split_step, Am, 2)
                        if not (isinstance(Am.n, int) and Am.n < 2):
                            dve.wait_ge(mT_ps, Am.n - 1)
                        dve.wait_ge(a_max, 12 * Am.n + 12)
                        step(v.tensor_copy(ms[Am.p][:, 0], mx[Am.p][:]))
                        v.tensor_tensor(ms[Am.p][:, 1], mx[Am.p][:], ms[Am.p][:, 0], ALU.subtract).then_inc(split_step, 1)
                        dve.wait_ge(mT_ps, Am.n + 1)
                        if not (isinstance(Am.n, int) and Am.n < 2):
                            dve.wait_ge(rows_in[Am.p], 16 * Am.half)
                        v.tensor_copy(mrow[Am.p][:], psM[0:64, 0:64].bitcast(bf16)).then_inc(mT_sb, 1)
                    if u == 7 and B:
                        normalise(B, 2)

            def layer_norm(s):
                v.tensor_tensor(y[:], psM[:, 0:T].rearrange("p (t d) -> p t d", t=2), xr[s.p][:], ALU.add
                                ).then_inc(y_sb, 1)
                dve.wait_ge(y_sb, s.n + 1)
                step = Steps(dve, ln_step, s, 2)
                for t in range(2):
                    ins = v.bn_stats(st[:, t, :], y[:, t, :])
                step(ins)
                hold(A, dve)
                for t in range(2):
                    ins = v.bn_aggr(mv[:, t, :], st[:, t, :])
                step(ins)
                v.tensor_scalar(vareps[:], mv[:, :, 1:2], EPS, None, ALU.add).then_inc(var_sb, 1)

            def scale_x1(s):
                dve.wait_ge(rstd_sb, s.n + 1)
                if not (isinstance(s.n, int) and s.n < 2):
                    dve.wait_ge(x1_out[s.p], 16 * s.half)
                    dve.wait_ge(x1T_ps, s.n - 1)
                for t in range(2):
                    ins = v.tensor_scalar(x1[s.p][:, t, :], y[:, t, :], mv[:, t, 0:1], rstd[:, t, :],
                                          ALU.subtract, ALU.mult)
                ins.then_inc(x1_sb, 1)

            iterations(dve, body)

        work.close()
        with nc.Block() as block:
            @block.gpsimd
            def _(pool):
                for s in used:
                    pool.sem_clear(s)


E8 = 8
NS = NTOK // 128 + E8
F0 = 512


def rank_tokens(nc, pe, ps, ones, below, hot, done, start_wait=None):
    mm = nc.tensor.matmul
    for t in range(NT):
        n = NT - t
        src = hot[:, t, :].unsqueeze(1).broadcast_to([128, n, E8])
        last = mm(ps[:, t + 1:NT + 1, :], ones[:], src, start=(t == 0), stop=True, skip_group_check=True)
    mm(ps[:, 0:NT, :], below[:], hot[:], start=False, stop=True, skip_group_check=True).then_inc(done, 1)


def route0(nc, A, x1d, xs, logits, slot, tile_expert, early):
    ctx = ExitStack()
    with ctx:
        def sb(name, shape, dt=f32):
            return ctx.enter_context(nc.sbuf_tensor("r0_" + name, shape, dt))

        def sem(name):
            return ctx.enter_context(nc.semaphore("r0_" + name))
        top = sb("top", [128, NT, 1])
        same = sb("same", [128, NT, E8])
        first = sb("first", [128, NT, 1])
        hot = sb("hot", [128, NT, E8], bf16)
        eid = sb("eid", [128, NT, E8])
        tid = sb("tid", [128, NS, E8])
        cnt = sb("cnt", [128, E8], i32)
        tiles = sb("tiles", [128, E8])
        ends = sb("ends", [128, E8])
        base = sb("base", [128, 1, E8])
        place = sb("place", [128, NT, E8])
        slotf = sb("slotf", [128, NT, 1])
        past = sb("past", [128, NS, E8])
        texp = sb("texp", [128, NS, 1])
        xall = sb("xall", [128, NT, D])
        ps = ctx.enter_context(nc.psum_tensor("r0_ps", [128, 512], f32))
        rank = ps[:, 0:(NT + 1) * E8].rearrange("p (t e) -> p t e", e=E8)
        iotas, step, hot_sb, ranked, slots_sb, x_in, scattered = (
            sem(n) for n in ("iotas", "step", "hot_sb", "ranked", "slots_sb", "x_in", "scattered"))
        block = ctx.enter_context(nc.Block())

        @block.sync
        def _(sp):
            xv = x1d.rearrange("(t p) d -> p t d", p=128)
            sp.dma_start(xall[:], xv).then_inc(x_in, 16)

        @block.gpsimd
        def _(pool):
            g = nc.gpsimd
            g.iota(eid[:], pattern=[[0, NT], [1, E8]], base=-E8, channel_multiplier=0,
                   allow_small_or_imprecise_dtypes=True)
            g.iota(tid[:], pattern=[[1, NS], [0, E8]], base=0, channel_multiplier=0,
                   allow_small_or_imprecise_dtypes=True).then_inc(iotas, 1)
            pool.wait_ge(x_in, 16)
            pool.wait_ge(slots_sb, 1)
            pool.wait_ge(early, 48)
            for t in range(NT):
                pool.indirect_dma_start(xs, bass.IndirectOffsetOnAxis(ap=slot[:, t:t + 1], axis=0),
                                        xall[:, t, :], None).then_inc(scattered, 16)
            pool.wait_ge(scattered, 16 * NT)

        @block.tensor
        def _(pe):
            pe.wait_ge(hot_sb, 1)
            rank_tokens(nc, pe, rank, A["onesb"], A["below"], hot, ranked)

        @block.vector
        def _(dve):
            v = nc.vector
            n = [0]

            def link(ins):
                n[0] += 1
                ins.then_inc(step, 1)
                dve.wait_ge(step, n[0])
            full = [128, NT, E8]
            link(v.tensor_reduce(top[:], logits[:], AX.X, ALU.max))
            link(v.tensor_tensor(same[:], logits[:], top[:].broadcast_to(full), ALU.is_equal))
            dve.wait_ge(iotas, 1)
            link(v.scalar_tensor_tensor(same[:], same[:], -float(E8), eid[:], ALU.mult, ALU.add))
            link(v.tensor_reduce(first[:], same[:], AX.X, ALU.min))
            v.scalar_tensor_tensor(hot[:], eid[:], -float(E8), first[:].broadcast_to(full), ALU.add,
                                   ALU.is_equal).then_inc(hot_sb, 1)
            dve.wait_ge(hot_sb, 1)
            dve.wait_ge(ranked, 1)
            link(v.tensor_scalar(cnt[:], rank[:, NT, :], 127.0, None, ALU.add))
            link(v.tensor_scalar(cnt[:], cnt[:], 7, None, ALU.logical_shift_right))
            link(v.tensor_copy(tiles[:], cnt[:]))
            link(v.tensor_tensor_scan(ends[:], A["ones"][:, 0:E8], tiles[:], 0.0, ALU.mult, ALU.add))
            link(v.tensor_tensor(base[:, 0, :], ends[:], tiles[:], ALU.subtract))
            link(v.scalar_tensor_tensor(place[:], base[:].broadcast_to(full), 128.0, rank[:, 0:NT, :], ALU.mult, ALU.add))
            link(v.tensor_tensor(place[:], place[:], hot[:], ALU.mult))
            link(v.tensor_reduce(slotf[:], place[:], AX.X, ALU.add))
            v.tensor_copy(slot[:], slotf[:, :, 0]).then_inc(slots_sb, 1)
            link(v.tensor_tensor(past[:], tid[:], ends[:].unsqueeze(1).broadcast_to([128, NS, E8]), ALU.is_ge))
            link(v.tensor_reduce(texp[:], past[:], AX.X, ALU.add))
            link(v.tensor_scalar(tile_expert[:], texp[:, :, 0], float(E8 - 1), None, ALU.min))


def experts0(nc, A, xs, ys, fc, pj, tile_expert):
    ctx = ExitStack()
    with ctx:
        def sb(name, shape, dt=f32):
            return ctx.enter_context(nc.sbuf_tensor("e0_" + name, shape, dt))

        def sem(name):
            return ctx.enter_context(nc.semaphore("e0_" + name))
        xt = [sb(f"xt{q}", [128, D]) for q in range(4)]
        xT = [sb(f"xT{p}", [D, 128]) for p in range(2)]
        w1 = [sb(f"w1{q}", [D, F0]) for q in range(4)]
        hr = [sb(f"hr{p}", [128, F0]) for p in range(2)]
        hT = [sb(f"hT{p}", [128, 4, 128]) for p in range(2)]
        yt = [sb(f"yt{q}", [128, D]) for q in range(4)]
        psX = [ctx.enter_context(nc.psum_tensor(f"e0_psX{p}", [128, 512], f32)) for p in range(2)]
        psH = [ctx.enter_context(nc.psum_tensor(f"e0_psH{p}", [128, 512], f32)) for p in range(2)]
        psY = [ctx.enter_context(nc.psum_tensor(f"e0_psY{p}", [128, 512], f32)) for p in range(2)]
        x_in = [sem(f"x_in{q}") for q in range(4)]
        y_out = [sem(f"y_out{q}") for q in range(4)]
        xT_ps, xT_sb, w1_sb, h_ps, relu_sb, h_sb, y_ps, y_sb = (
            sem(n) for n in ("xT_ps", "xT_sb", "w1_sb", "h_ps", "relu_sb", "h_sb", "y_ps", "y_sb"))
        block = ctx.enter_context(nc.Block())

        def tiles(eng, body):
            for k in range(4):
                body(Quad(0, k))
            with eng.Fori(1, NS // 4) as j:
                for k in range(4):
                    body(Quad(j, k))


        @block.sync
        def _(sp):
            xv = xs.rearrange("(s p) d -> s p d", p=128)
            yv = ys.rearrange("(s p) d -> s p d", p=128)

            def body(s):
                if later(s, 4):
                    sp.wait_ge(xT_ps, s.n - 3)
                sp.dma_start(xt[s.q][:], xv[s.n]).then_inc(x_in[s.q], 16)
                if later(s, 4):
                    store(Quad(s.four - 1, s.q))

            def store(s):
                sp.wait_ge(y_sb, s.n + 1)
                sp.dma_start(yv[s.n], yt[s.q][:]).then_inc(y_out[s.q], 16)
            tiles(sp, body)
            for k in range(4):
                store(Quad(NS // 4 - 1, k))
            for q in range(4):
                sp.wait_ge(y_out[q], 16 * (NS // 4))

        @block.gpsimd
        def _(pool):
            def body(s):
                e = pool.value_load(tile_expert[0:1, bass.ds(s.n, 1)], min_val=0, max_val=E8 - 1)
                if later(s, 4):
                    pool.wait_ge(h_ps, s.n - 3)
                nc.gpsimd.tensor_copy(w1[s.q][:], fc[:, bass.ds(e, 1), :].rearrange("p o f -> p (o f)")).then_inc(w1_sb, 1)
            tiles(pool, body)

        @block.tensor
        def _(pe):
            mm = nc.tensor.matmul

            def transpose(s):
                pe.wait_ge(x_in[s.q], 16 * (s.four + 1))
                if later(s):
                    pe.wait_ge(xT_sb, s.n - 1)
                nc.tensor.transpose(psX[s.p][:, 0:128], xt[s.q][:], A["ident"][:]).then_inc(xT_ps, 1)

            def up(s):
                pe.wait_ge(xT_sb, s.n + 1)
                pe.wait_ge(w1_sb, s.n + 1)
                if later(s):
                    pe.wait_ge(relu_sb, s.n - 1)
                for c in range(4):
                    last = mm(psH[s.p][:, 128 * c:128 * c + 128], w1[s.q][:, 128 * c:128 * c + 128], xT[s.p][:],
                              start=True, stop=True)
                last.then_inc(h_ps, 1)

            def down(s):
                e = pe.value_load(tile_expert[0:1, bass.ds(s.n, 1)], min_val=0, max_val=E8 - 1)
                pe.wait_ge(h_sb, s.n + 1)
                if later(s):
                    pe.wait_ge(y_sb, s.n - 1)
                for c in range(4):
                    last = mm(psY[s.p][:, 0:D], hT[s.p][:, c, :], pj[:, bass.ds(e, 1), c, :].rearrange("p o d -> p (o d)"),
                              start=(c == 0), stop=(c == 3))
                last.then_inc(y_ps, 1)

            transpose(Quad(0, 0))
            transpose(Quad(0, 1))
            up(Quad(0, 0))

            def round(j, last=False):
                for k in range(4):
                    if not last or k < 2:
                        transpose(Quad(j, k + 2))
                    if not last or k < 3:
                        up(Quad(j, k + 1))
                    down(Quad(j, k))
            round(0)
            with pe.Fori(1, NS // 4 - 1) as j:
                round(j)
            round(NS // 4 - 1, True)

        @block.scalar
        def _(act):
            def copy_x(s):
                act.wait_ge(xT_ps, s.n + 1)
                if later(s):
                    act.wait_ge(h_ps, s.n - 1)
                nc.scalar.copy(xT[s.p][:], psX[s.p][:, 0:128]).then_inc(xT_sb, 1)

            def relu(s):
                act.wait_ge(h_ps, s.n + 1)
                if later(s):
                    act.wait_ge(h_sb, s.n - 1)
                nc.scalar.activation(hr[s.p][:], psH[s.p][:], ACT.Relu).then_inc(relu_sb, 1)

            def out(s):
                act.wait_ge(y_ps, s.n + 1)
                if later(s, 4):
                    act.wait_ge(y_out[s.q], 16 * s.four)
                nc.scalar.copy(yt[s.q][:], psY[s.p][:, 0:D]).then_inc(y_sb, 1)
            copy_x(Quad(0, 0))
            copy_x(Quad(0, 1))
            relu(Quad(0, 0))

            def round(j, last=False):
                for k in range(4):
                    if not last or k < 2:
                        copy_x(Quad(j, k + 2))
                    if not last or k < 3:
                        relu(Quad(j, k + 1))
                    out(Quad(j, k))
            round(0)
            with act.Fori(1, NS // 4 - 1) as j:
                round(j)
            round(NS // 4 - 1, True)

        @block.vector
        def _(dve):
            def body(s):
                dve.wait_ge(relu_sb, s.n + 1)
                if later(s):
                    dve.wait_ge(y_ps, s.n - 1)
                r = hr[s.p][:]
                nc.vector.tensor_tensor(hT[s.p][:].rearrange("p c t -> p (c t)"), r, r, ALU.mult).then_inc(h_sb, 1)
            tiles(dve, body)


H1 = 4
DH1 = D // H1
WINDOWS = [4, 16, 64, 32]
FAR = 1e9
W1 = T + 128

def attention1(nc, A, x1d, ys, slot, wqkvT, qkvb_col, qkvb_row, offT, lin2T, lin2b, gateT, x3d, acc, logits, NB=NB):
    ctx = ExitStack()
    with ctx:
        def sb(name, shape, dt=f32):
            return ctx.enter_context(nc.sbuf_tensor("a1_" + name, shape, dt))

        def sem(name):
            return ctx.enter_context(nc.semaphore("a1_" + name))
        ident, identb = A["ident"], A["identb"]
        wq = sb("wq", [D, 3 * D])
        bcol = sb("bcol", [D, 3])
        bq8 = sb("bq8", [D, 1])
        brow = sb("brow", [128, D])
        wof = sb("wof", [D, 32])
        wl = sb("wl", [32, 1])
        nb = sb("nb", [128, 1])
        wg = sb("wg", [D, E8])
        dif = sb("dif", [128, W1], bf16)
        win = sb("win", [128, 2, H1])
        x1t = [sb(f"x1t{p}", [128, 2, D]) for p in range(2)]
        ix = [sb(f"ix{p}", [128, 2], i32) for p in range(2)]
        yg = [sb(f"yg{p}", [128, 2, D]) for p in range(2)]
        z = sb("z", [128, 2, D])
        st = sb("st", [128, 2, 6])
        mv = sb("mv", [128, 2, 2])
        ve, rs = sb("ve", [128, 2, 1]), sb("rs", [128, 2, 1])
        ve3, rs3 = sb("ve3", [128, 2, 1]), sb("rs3", [128, 2, 1])
        x2 = [sb(f"x2{p}", [128, 2, D]) for p in range(2)]
        x2all = sb("x2all", [128, NT, D])
        x2T, r2T = sb("x2T", [D, T]), sb("r2T", [D, T])
        qT = [sb(f"qT{p}", [D, T]) for p in range(2)]
        kT = [sb(f"kT{p}", [D, T]) for p in range(2)]
        va = [sb(f"va{p}", [128, 2, H1, 64]) for p in range(2)]
        o32 = sb("o32", [32, T])
        zc, ez, dx0, dx1 = sb("zc", [128, 2]), sb("ez", [128, 2]), sb("dx0", [128, 2]), sb("dx1", [128, 2, 1])
        dxh = sb("dxh", [128, 2, H1])
        mk = [sb(f"mk{p}", [128, H1, W1], bf16) for p in range(2)]
        mb = sb("mb", [128, H1, W1], bf16)
        nm = sb("nm", [128, 2, H1])
        pr = [sb(f"pr{p}", [128, W1]) for p in range(2)]
        oT = sb("oT", [128, 2 * T])
        rc = sb("rc", [128, 2, H1])
        att = sb("att", [128, 2, D])
        y3 = sb("y3", [128, 2, D])
        st3, mv3 = sb("st3", [128, 2, 6]), sb("mv3", [128, 2, 2])
        x3 = [sb(f"x3{p}", [128, 2, D]) for p in range(2)]
        twice = [sb(f"twice{p}", [128, 2, D]) for p in range(2)]
        x3T = sb("x3T", [D, T])
        psA = [ctx.enter_context(nc.psum_tensor(f"a1_psA{p}", [128, 512], f32)) for p in range(2)]
        psB = [ctx.enter_context(nc.psum_tensor(f"a1_psB{p}", [128, 512], f32)) for p in range(2)]
        psO = ctx.enter_context(nc.psum_tensor("a1_psO", [128, 512], f32))
        psM = ctx.enter_context(nc.psum_tensor("a1_psM", [128, 512], f32))
        psP = ctx.enter_context(nc.psum_tensor("a1_psP", [128, 512], f32))
        psZ = ctx.enter_context(nc.psum_tensor("a1_psZ", [128, 512], f32))
        w_in, consts, consts_step, bias_sb = sem("w_in"), sem("consts"), sem("consts_step"), sem("bias_sb")
        x1_in = [sem(f"x1_in{p}") for p in range(2)]
        y_in = [sem(f"y_in{p}") for p in range(2)]
        x3_out = [sem(f"x3_out{p}") for p in range(2)]
        (twice_sb, ix_sb, zc_sb, z_sb, n_step, var2, rstd2, x2_sb, x2_kept, x2T_ps, x2T_sb, r2T_sb, qk_ps, qk_sb, v_ps, v_sb, off_ps, off_sb,
         z_ps, ez_sb, dx_step, mask_sb, a_ps, a_max, shift_sb, s_ps, probs, pv_done, o_sb, otr_ps, f_step, y3_sb,
         var3, rstd3, x3_sb, x3T_ps, x3T_sb, g_ps, g_sb) = (
            sem(n) for n in "twice_sb ix_sb zc_sb z_sb n_step var2 rstd2 x2_sb x2_kept x2T_ps x2T_sb r2T_sb qk_ps qk_sb v_ps v_sb off_ps "
            "off_sb z_ps ez_sb dx_step mask_sb a_ps a_max shift_sb s_ps probs pv_done o_sb otr_ps f_step y3_sb var3 "
            "rstd3 x3_sb x3T_ps x3T_sb g_ps g_sb".split())
        block = ctx.enter_context(nc.Block())

        def iterations(eng, body):
            def peeled(i):
                def seq(off):
                    return Seq(0, i + off) if 0 <= i + off < NB else None
                body(seq(-1), seq(0), seq(1), seq(2))
            for i in range(-2, 2):
                peeled(i)
            with eng.Fori(1, 1 + (NB - 4) // 2) as j:
                for k in range(2):
                    body(Seq(j, k - 1) if k else Seq(j - 1, 1), Seq(j, k), Seq(j, k + 1), Seq(j, k + 2))
            for i in range(NB - 2, NB + 1):
                peeled(i)

        @block.sync
        def _(sp):
            for dst, src in ((wq, wqkvT), (bcol, qkvb_col), (wof, offT), (wl, lin2T), (wg, gateT)):
                sp.dma_start(dst[:], src).then_inc(w_in, 16)
            sp.dma_start(brow[:], qkvb_row.broadcast_to([128, D])).then_inc(w_in, 16)
            sp.dma_start(nb[:], lin2b.broadcast_to([128, 1])).then_inc(w_in, 16)
            x1v = x1d.rearrange("(b t p) d -> b p t d", t=2, p=128)
            accv = acc.rearrange("(b t p) d -> b p t d", t=2, p=128)
            x3v = x3d.rearrange("(b t p) d -> b p t d", t=2, p=128)

            def body(F, C, P, N):
                if N:
                    if later(N):
                        sp.wait_ge(z_sb, N.n - 1)
                    sp.dma_start(x1t[N.p][:], x1v[N.n]).then_inc(x1_in[N.p], 16)
                if F:
                    sp.wait_ge(x3_sb, F.n + 1)
                    sp.dma_start(x3v[F.n], x3[F.p][:]).then_inc(x3_out[F.p], 16)
                    sp.wait_ge(twice_sb, F.n + 1)
                    sp.dma_start(accv[F.n], twice[F.p][:]).then_inc(x3_out[F.p], 16)
            iterations(sp, body)
            for p in range(2):
                sp.wait_ge(x3_out[p], 32 * (NB // 2))

        @block.gpsimd
        def _(pool):
            g = nc.gpsimd
            g.iota(dif[:, 0:T], pattern=[[1, T]], base=0, channel_multiplier=-1, allow_small_or_imprecise_dtypes=True)
            g.iota(dif[:, T:W1], pattern=[[1, 128]], base=0, channel_multiplier=-1,
                   allow_small_or_imprecise_dtypes=True)
            for i, w in enumerate(WINDOWS):
                g.memset(win[:, :, i], float(w))
            for p in range(2):
                last = g.memset(va[p][:], 1.0)
            last.then_inc(consts_step, 1)
            pool.wait_ge(consts_step, 1)
            g.affine_select(out=dif[:, 0:T], in_=dif[:, 0:T], pattern=[[1, T]], compare_op=ALU.is_ge, fill=FAR,
                            base=0, channel_multiplier=-1)
            g.affine_select(out=dif[:, T:W1], in_=dif[:, T:W1], pattern=[[1, 128]], compare_op=ALU.is_ge, fill=FAR,
                            base=0, channel_multiplier=-1).then_inc(consts, 1)

            def body(F, C, P, N):
                if N:
                    if later(N):
                        pool.wait_ge(z_sb, N.n - 1)
                        pool.wait_ge(y_in[N.p], 32 * N.half)
                    g.tensor_copy(ix[N.p][:], slot[:, bass.ds(2 * N.n, 2)]).then_inc(ix_sb, 1)
                    pool.wait_ge(ix_sb, N.n + 1)
                    hold(A, pool)
                    for t in range(2):
                        pool.indirect_dma_start(yg[N.p][:, t, :], None, ys, bass.IndirectOffsetOnAxis(
                            ap=ix[N.p][:, t:t + 1], axis=0)).then_inc(y_in[N.p], 16)
                if F:
                    pool.wait_ge(var3, F.n + 1)
                    g.tensor_tensor(rs3[:], ve3[:], A["mhalf"][:, 0:2], ALU.pow).then_inc(rstd3, 1)
                if N:
                    pool.wait_ge(var2, N.n + 1)
                    g.tensor_tensor(rs[:], ve[:], A["mhalf"][:, 0:2], ALU.pow).then_inc(rstd2, 1)
                    pool.wait_ge(x2_sb, N.n + 1)
                    g.tensor_copy(x2all[:, bass.ds(2 * N.n, 2), :], x2[N.p][:]).then_inc(x2_kept, 1)
            iterations(pool, body)

        @block.tensor
        def _(pe):
            mm = nc.tensor.matmul
            pe.wait_ge(w_in, 16 * 7)
            pe.wait_ge(consts, 1)

            def scores_for_max(s, h):
                if h == 0:
                    pe.wait_ge(mask_sb, s.n + 1)
                    pe.wait_ge(qk_sb, s.n + 1)
                if later(s, 1) or h >= 2:
                    pe.wait_ge(a_max, 4 * s.n + h - 1)
                r = slice(32 * h, 32 * h + 32)
                mm(psA[h % 2][:, 0:W1], identb[:], mk[s.p][:, h, :], start=True, stop=True)
                mm(psA[h % 2][:, 0:T], qT[s.p][r, 0:128], kT[s.p][r, :], start=False, stop=True,
                   skip_group_check=True, tile_position=(32 * h, 0))
                mm(psA[h % 2][:, T:W1], qT[s.p][r, 128:T], kT[s.p][r, 128:T], start=False, stop=True,
                   skip_group_check=True, tile_position=(32 * h, 0)).then_inc(a_ps, 1)

            def scores(s, h):
                pe.wait_ge(shift_sb, 4 * s.n + h + 1)
                if later(s, 1) or h >= 2:
                    pe.wait_ge(probs, 4 * s.n + h - 1)
                r = slice(32 * h, 32 * h + 32)
                b = psB[h % 2]
                for c in range(3):
                    cols = slice(128 * c, 128 * c + 128)
                    mm(b[:, cols], mb[:, h, cols], identb[:], start=(c == 0), stop=True, skip_group_check=True)
                mm(b[:, 0:128], kT[s.p][r, 0:128], qT[s.p][r, 0:128], start=False, stop=True,
                   skip_group_check=True, tile_position=(32 * h, 0))
                mm(b[:, 128:W1], kT[s.p][r, 128:T], qT[s.p][r, :], start=False, stop=True,
                   skip_group_check=True, tile_position=(32 * h, 0)).then_inc(s_ps, 1)

            def weigh_values(s, h):
                pe.wait_ge(probs, 4 * s.n + h + 1)
                if h == 0:
                    pe.wait_ge(v_sb, s.n + 1)
                    if later(s, 1):
                        pe.wait_ge(o_sb, s.n)
                rows = slice(64 * (h % 2), 64 * (h % 2) + 64)
                c0 = T * (h // 2)
                mm(psO[rows, c0:c0 + T], va[s.p][:, 1, h, :], pr[h % 2][:, 128:W1], start=True, stop=True,
                   tile_position=(0, 64 * (h % 2)))
                mm(psO[rows, c0:c0 + 128], va[s.p][:, 0, h, :], pr[h % 2][:, 0:128], start=False, stop=True,
                   skip_group_check=True, tile_position=(0, 64 * (h % 2))).then_inc(pv_done, 1)

            def tr2(ps, src):
                for t in range(2):
                    last = nc.tensor.transpose(ps[:, 128 * t:128 * t + 128], src[:, t, :], ident[:])
                return last

            def body(F, C, P, N):
                if C:
                    scores_for_max(C, 0)
                    scores_for_max(C, 1)
                if F:
                    pe.wait_ge(o_sb, F.n + 1)
                    if later(F, 1):
                        pe.wait_ge(g_sb, F.n)
                    for t in range(2):
                        for hp in range(2):
                            last = nc.tensor.transpose(psM[:, 256 * t + 128 * hp:256 * t + 128 * hp + 128],
                                                       oT[:, T * hp + 128 * t:T * hp + 128 * t + 128], ident[:])
                    last.then_inc(otr_ps, 1)
                if P:
                    pe.wait_ge(x2_sb, P.n + 1)
                    if later(P, 1):
                        pe.wait_ge(off_sb, P.n)
                    tr2(psP, x2[P.p]).then_inc(x2T_ps, 1)
                if C:
                    scores_for_max(C, 2)
                    scores_for_max(C, 3)
                    scores(C, 0)
                if P:
                    pe.wait_ge(x2T_sb, P.n + 1)
                    pe.wait_ge(r2T_sb, P.n + 1)
                    for c in range(2):
                        last = mm(psP[:, T * c:T * c + T], wq[:, D * c:D * c + D], x2T[:], start=True, stop=True)
                    last.then_inc(qk_ps, 1)
                    if later(P, 1):
                        pe.wait_ge(ez_sb, P.n)
                    mm(psZ[0:32, 0:T], wof[:], r2T[:], start=True, stop=True).then_inc(off_ps, 1)
                if C:
                    scores(C, 1)
                    weigh_values(C, 0)
                if F:
                    pe.wait_ge(x3_sb, F.n + 1)
                    tr2(psM, x3[F.p]).then_inc(x3T_ps, 1)
                if P:
                    pe.wait_ge(qk_sb, P.n + 1)
                    for t in range(2):
                        last = mm(psP[:, D * t:D * t + D], x2T[:, 128 * t:128 * t + 128], wq[:, 2 * D:3 * D],
                                  start=True, stop=True)
                    last.then_inc(v_ps, 1)
                    pe.wait_ge(off_sb, P.n + 1)
                    for t in range(2):
                        last = mm(psZ[:, T + t:T + t + 1], o32[:, 128 * t:128 * t + 128], wl[:], start=True, stop=True)
                    last.then_inc(z_ps, 1)
                if C:
                    scores(C, 2)
                    weigh_values(C, 1)
                if C:
                    scores(C, 3)
                    weigh_values(C, 2)
                if F:
                    pe.wait_ge(x3T_sb, F.n + 1)
                    for t in range(2):
                        last = mm(psM[:, E8 * t:E8 * t + E8], x3T[:, 128 * t:128 * t + 128], wg[:], start=True,
                                  stop=True)
                    last.then_inc(g_ps, 1)
                if P:
                    pe.wait_ge(v_sb, P.n + 1)
                if C:
                    weigh_values(C, 3)
            iterations(pe, body)

        @block.scalar
        def _(act):
            a = nc.scalar
            act.wait_ge(w_in, 16 * 7)
            a.mul(bq8[:], bcol[:, 0:1], 2.0 * T ** -0.5).then_inc(bias_sb, 1)
            act.wait_ge(bias_sb, 1)

            def exps(s, h):
                act.wait_ge(s_ps, 4 * s.n + h + 1)
                if later(s, 1) or h >= 2:
                    act.wait_ge(pv_done, 4 * s.n + h - 1)
                a.activation(pr[h % 2][:], psB[h % 2][:, 0:W1], ACT.Exp).then_inc(probs, 1)

            def body(F, C, P, N):
                if F:
                    act.wait_ge(pv_done, 4 * F.n + 4)
                    if later(F, 1):
                        act.wait_ge(otr_ps, F.n)
                    a.copy(oT[:], psO[:]).then_inc(o_sb, 1)
                if P:
                    act.wait_ge(x2T_ps, P.n + 1)
                    if later(P, 1):
                        act.wait_ge(off_ps, P.n)
                    a.copy(x2T[:], psP[:, 0:T]).then_inc(x2T_sb, 1)
                    a.activation(r2T[:], psP[:, 0:T], ACT.Relu).then_inc(r2T_sb, 1)
                if C:
                    exps(C, 0)
                if P:
                    act.wait_ge(qk_ps, P.n + 1)
                    if later(P):
                        act.wait_ge(s_ps, 4 * P.n - 4)
                    a.activation(qT[P.p][:], psP[:, 0:T], ACT.Identity, bias=bq8[:], scale=2.0 * T ** -0.5)
                    a.activation(kT[P.p][:], psP[:, T:2 * T], ACT.Identity, bias=bcol[:, 1:2]).then_inc(qk_sb, 1)
                if C:
                    exps(C, 1)
                if P:
                    act.wait_ge(off_ps, P.n + 1)
                    a.copy(o32[:], psZ[0:32, 0:T]).then_inc(off_sb, 1)
                if F:
                    act.wait_ge(x3T_ps, F.n + 1)
                    a.copy(x3T[:], psM[:, 0:T]).then_inc(x3T_sb, 1)
                    if later(F):
                        act.wait_ge(x3_out[F.p], 32 * F.half)
                    a.mul(twice[F.p][:], x3[F.p][:], 2.0).then_inc(twice_sb, 1)
                if C:
                    exps(C, 2)
                if P:
                    act.wait_ge(zc_sb, P.n + 1)
                    if later(P, 1):
                        act.wait_ge(mask_sb, P.n)
                    a.activation(ez[:], zc[:], ACT.Exp, scale=-1.0).then_inc(ez_sb, 1)
                if C:
                    exps(C, 3)
            iterations(act, body)

        @block.vector
        def _(dve):
            v = nc.vector

            def norm(step, src, st, mv, ve, var):
                for t in range(2):
                    ins = v.bn_stats(st[:, t, :], src[:, t, :])
                step(ins)
                hold(A, dve)
                for t in range(2):
                    ins = v.bn_aggr(mv[:, t, :], st[:, t, :])
                step(ins)
                v.tensor_scalar(ve[:], mv[:, :, 1:2], EPS, None, ALU.add).then_inc(var, 1)

            def maximum(s, h):
                dve.wait_ge(a_ps, 4 * s.n + h + 1)
                if later(s, 1) or h > 0:
                    dve.wait_ge(shift_sb, 4 * s.n + h)
                v.tensor_reduce(nm[:, 0, h:h + 1], psA[h % 2][:, 0:T], AX.X, ALU.max, negate=True)
                v.tensor_reduce(nm[:, 1, h:h + 1], psA[h % 2][:, T:W1], AX.X, ALU.max, negate=True).then_inc(a_max, 1)
                dve.wait_ge(a_max, 4 * s.n + h + 1)
                if later(s, 1):
                    dve.wait_ge(s_ps, 4 * s.n - 3 + h)
                v.tensor_scalar(mb[:, h, 0:T], mk[s.p][:, h, 0:T], nm[:, 0, h:h + 1], None, ALU.add)
                v.tensor_scalar(mb[:, h, T:W1], mk[s.p][:, h, T:W1], nm[:, 1, h:h + 1], None, ALU.add
                                ).then_inc(shift_sb, 1)

            def body(F, C, P, N):
                if C:
                    maximum(C, 0)
                    maximum(C, 1)
                if F:
                    step = Steps(dve, f_step, F, 4)
                    dve.wait_ge(otr_ps, F.n + 1)
                    o = psM[:].rearrange("p (t h r) -> p t h r", t=2, r=64)
                    step(v.reciprocal(rc[:], o[:, :, :, DH1]))
                    step(v.tensor_tensor(att[:].rearrange("p t (h d) -> p t h d", d=DH1), o[:, :, :, 0:DH1],
                                         rc[:].unsqueeze(3).broadcast_to([128, 2, H1, DH1]), ALU.mult))
                    dve.wait_ge(x2_kept, F.n + 1)
                    v.tensor_tensor(y3[:], att[:], x2all[:, bass.ds(2 * F.n, 2), :], ALU.add).then_inc(y3_sb, 1)
                    dve.wait_ge(y3_sb, F.n + 1)
                    norm(step, y3, st3, mv3, ve3, var3)
                if C:
                    maximum(C, 2)
                if F:
                    dve.wait_ge(rstd3, F.n + 1)
                    if later(F):
                        dve.wait_ge(x3_out[F.p], 32 * F.half)
                    for t in range(2):
                        ins = v.tensor_scalar(x3[F.p][:, t, :], y3[:, t, :], mv3[:, t, 0:1], rs3[:, t, :],
                                              ALU.subtract, ALU.mult)
                    ins.then_inc(x3_sb, 1)
                if C:
                    maximum(C, 3)
                if P:
                    dve.wait_ge(v_ps, P.n + 1)
                    if later(P):
                        dve.wait_ge(pv_done, 4 * P.n - 4)
                    for t in range(2):
                        ins = v.tensor_tensor(va[P.p][:, t, :, 0:DH1],
                                              psP[:, D * t:D * t + D].rearrange("p (h d) -> p h d", d=DH1),
                                              brow[:].rearrange("p (h d) -> p h d", d=DH1), ALU.add)
                    ins.then_inc(v_sb, 1)
                if P:
                    step = Steps(dve, dx_step, P, 3)
                    dve.wait_ge(z_ps, P.n + 1)
                    v.tensor_scalar(zc[:], psZ[:, T:T + 2], nb[:], -80.0, ALU.add, ALU.max).then_inc(zc_sb, 1)
                    dve.wait_ge(ez_sb, P.n + 1)
                    step(v.tensor_scalar(dx0[:], ez[:], 1.0, None, ALU.add))
                    step(v.reciprocal(dx1[:, :, 0], dx0[:]))
                    step(v.scalar_tensor_tensor(dxh[:], dx1[:].broadcast_to([128, 2, H1]), float(T), win[:],
                                                ALU.mult, ALU.add))
                    for h in range(H1):
                        for t, cols in ((0, slice(0, T)), (1, slice(T, W1))):
                            ins = v.tensor_scalar(mk[P.p][:, h, cols], dif[:, cols], dxh[:, t, h:h + 1], -BIG,
                                                  ALU.is_gt, ALU.mult)
                    ins.then_inc(mask_sb, 1)
                if F:
                    dve.wait_ge(g_ps, F.n + 1)
                    v.tensor_copy(logits[:, bass.ds(2 * F.n, 2), :],
                                  psM[:, 0:16].rearrange("p (t e) -> p t e", e=E8)).then_inc(g_sb, 1)
                if N:
                    dve.wait_ge(x1_in[N.p], 16 * (N.half + 1))
                    dve.wait_ge(y_in[N.p], 32 * (N.half + 1))
                    v.tensor_tensor(z[:], x1t[N.p][:], yg[N.p][:], ALU.add).then_inc(z_sb, 1)
                    dve.wait_ge(z_sb, N.n + 1)
                    step = Steps(dve, n_step, N, 2)
                    norm(step, z, st, mv, ve, var2)
                    dve.wait_ge(rstd2, N.n + 1)
                    if later(N):
                        dve.wait_ge(x2T_ps, N.n - 1)
                        dve.wait_ge(x2_kept, N.n - 1)
                    for t in range(2):
                        ins = v.tensor_scalar(x2[N.p][:, t, :], z[:, t, :], mv[:, t, 0:1], rs[:, t, :],
                                              ALU.subtract, ALU.mult)
                    ins.then_inc(x2_sb, 1)
            dve.wait_ge(w_in, 16 * 7)
            dve.wait_ge(consts, 1)
            iterations(dve, body)


CAP = NTOK // E8
SEG = 128 // E8
F1 = 4 * D


def choose1(nc, A, logits, scored, ids):
    ctx = ExitStack()
    with ctx:
        def sb(name, shape, dt=f32):
            return ctx.enter_context(nc.sbuf_tensor("c1_" + name, shape, dt))

        def sem(name):
            return ctx.enter_context(nc.semaphore("c1_" + name))

        def psum(name):
            return ctx.enter_context(nc.psum_tensor("c1_" + name, [128, 512], f32))
        full = [128, NT, E8]
        red = sb("red", [128, NT, 1])
        pb = sb("pb", full)
        byx = sb("byx", [128, 2, E8, SEG])
        sc = sb("sc", [128, T])
        ge = sb("ge", [128, T], bf16)
        cnt = sb("cnt", [128, 1])
        group = sb("group", [128, 128])
        lead = sb("lead", [128, E8])
        thr, cand, flag = sb("thr", [128, 1], i32), sb("cand", [128, 1], i32), sb("flag", [128, 1], i32)
        bit, thrf = sb("bit", [128, 1], i32), sb("thrf", [128, 1])
        thrrow = sb("thrrow", [128, 1, E8])
        gt, eq = sb("gt", full, bf16), sb("eq", full, bf16)
        need = sb("need", [128, 1, E8])
        eqr = sb("eqr", full)
        okk, sel, pos, posi, posh = sb("okk", full), sb("sel", full), sb("pos", full), sb("posi", full, i32), sb("posh", full)
        lo = sb("lo", full)
        it4 = sb("it4", [128, NT * E8, 4])
        tokp, tokt = sb("tokp", [128, 1]), sb("tokt", [128, NT, E8 * 4])
        hot4 = sb("hot4", [128, NT * E8, 4])
        val = sb("val", [128, NT, E8, 2, 4], bf16)
        lane = sb("lane", [128, 128], bf16)
        NHOT, GRP = 16, 8
        hot = sb("hot", [128, NHOT, 128], bf16)
        idf = sb("idf", [128, E8, 4])
        psT, psC, psE, psG, psI = psum("psT"), psum("psC"), psum("psE"), psum("psG"), psum("psI")
        (iotas, step, p_sb, p_exp, x_sb, t_ps, c_sb, c_ps, thr_sb, row_ps, mask_sb, ranked, val_sb, hot_sb, hot_used,
         t_step, pb_out, lanes) = (sem(n) for n in "iotas step p_sb p_exp x_sb t_ps c_sb c_ps thr_sb row_ps mask_sb "
                           "ranked val_sb hot_sb hot_used t_step pb_out lanes".split())
        block = ctx.enter_context(nc.Block())
        BITS = 30
        STEP = 6

        @block.sync
        def _(sp):
            sp.wait_ge(p_sb, 1)
            sp.dma_start(scored.rearrange("(t p) e -> p t e", p=128), pb[:]).then_inc(pb_out, 16)
            sp.wait_ge(pb_out, 16)

        @block.gpsimd
        def _(pool):
            g = nc.gpsimd
            g.memset(group[:], 1.0)
            g.memset(lead[:], 1.0)
            g.iota(it4[:], pattern=[[0, NT * E8], [1, 4]], base=0, channel_multiplier=0,
                   allow_small_or_imprecise_dtypes=True)
            g.iota(tokp[:], pattern=[[0, 1]], base=0, channel_multiplier=1, allow_small_or_imprecise_dtypes=True)
            g.iota(tokt[:], pattern=[[1, NT], [0, E8 * 4]], base=0, channel_multiplier=0,
                   allow_small_or_imprecise_dtypes=True)
            g.iota(lane[:], pattern=[[1, 128]], base=0, channel_multiplier=0,
                   allow_small_or_imprecise_dtypes=True).then_inc(lanes, 1)
            pool.wait_ge(lanes, 1)
            gv = group[:].rearrange("p (e s) -> p e s", s=SEG)
            g.affine_select(out=gv, in_=gv, pattern=[[-SEG, E8], [0, SEG]], compare_op=ALU.is_ge, fill=0.0,
                            base=0, channel_multiplier=1)
            g.affine_select(out=lead[:], in_=lead[:], pattern=[[-SEG, E8]], compare_op=ALU.is_equal, fill=0.0,
                            base=0, channel_multiplier=1).then_inc(lanes, 1)
            pool.wait_ge(lanes, 2)
            g.affine_select(out=gv, in_=gv, pattern=[[SEG, E8], [0, SEG]], compare_op=ALU.is_ge, fill=0.0,
                            base=SEG - 1, channel_multiplier=-1).then_inc(iotas, 1)

        @block.scalar
        def _(act):
            act.wait_ge(step, 2)
            nc.scalar.activation(pb[:], pb[:], ACT.Exp).then_inc(p_exp, 1)

        @block.tensor
        def _(pe):
            mm = nc.tensor.matmul
            pe.wait_ge(x_sb, 1)
            for u in range(2):
                last = nc.tensor.transpose(psT[:, 128 * u:128 * u + 128],
                                           byx[:, u].rearrange("p e s -> p (e s)"), A["ident"][:])
            last.then_inc(t_ps, 1)
            pe.wait_ge(iotas, 1)
            with pe.Fori(0, BITS // STEP) as j:
                for k in range(STEP):
                    pe.wait_ge(c_sb, STEP * j + k + 1)
                    mm(psC[:, 0:1], group[:], cnt[:], start=True, stop=True).then_inc(c_ps, 1)
            pe.wait_ge(thr_sb, 1)
            mm(psC[:, 8:16], thrf[:].broadcast_to([128, 128]), lead[:], start=True, stop=True).then_inc(row_ps, 1)
            pe.wait_ge(mask_sb, 1)
            rank_tokens(nc, pe, psE[:, 0:(NT + 1) * E8].rearrange("p (t e) -> p t e", e=E8), A["onesb"], A["below"], eq, ranked)
            rank_tokens(nc, pe, psG[:, 0:(NT + 1) * E8].rearrange("p (t e) -> p t e", e=E8), A["onesb"], A["below"], gt, ranked)
            pe.wait_ge(val_sb, 1)

            def place(e):
                for t in range(NT):
                    if t % GRP == 0:
                        pe.wait_ge(hot_sb, (NT // GRP) * e + t // GRP + 1)
                    last = mm(psI[:, bass.ds(8 * e, 8)], hot[:, t % NHOT, :], val[:, t, bass.ds(e, 1)].rearrange("p o c a -> p (o c a)"),
                       start=(t == 0), stop=(t == NT - 1))
                    if t % GRP == GRP - 1:
                        last.then_inc(hot_used, 1)
            place(0)
            with pe.Fori(1, E8) as e:
                place(e)

        @block.vector
        def _(dve):
            v = nc.vector
            n = [0]

            def link(ins):
                n[0] += 1
                ins.then_inc(step, 1)
                dve.wait_ge(step, n[0])
            link(v.tensor_reduce(red[:], logits[:], AX.X, ALU.max))
            link(v.tensor_tensor(pb[:], logits[:], red[:].broadcast_to(full), ALU.subtract))
            dve.wait_ge(p_exp, 1)
            link(v.tensor_reduce(red[:], pb[:], AX.X, ALU.add))
            link(v.reciprocal(red[:], red[:]))
            v.tensor_tensor(pb[:], pb[:], red[:].broadcast_to(full), ALU.mult).then_inc(p_sb, 1)
            dve.wait_ge(p_sb, 1)
            v.tensor_copy(byx[:], pb[:].rearrange("p (s u) e -> p u e s", u=2)).then_inc(x_sb, 1)
            dve.wait_ge(t_ps, 1)
            v.tensor_copy(sc[:], psT[:, 0:T])
            v.memset(thr[:], 0)
            link(v.memset(bit[:], 1 << (BITS - 1)))
            with dve.Fori(0, BITS // STEP) as j:
                for k in range(STEP):
                    i = STEP * j + k
                    v.tensor_tensor(cand[:], thr[:], bit[:], ALU.bitwise_or).then_inc(t_step, 1)
                    dve.wait_ge(t_step, 3 * i + 1)
                    v.tensor_scalar(ge[:], sc[:], cand[:].bitcast(f32), 0.0, ALU.is_ge, ALU.add, accum_out=cnt[:]
                                    ).then_inc(c_sb, 1)
                    v.tensor_scalar(bit[:], bit[:], 1, None, ALU.logical_shift_right)
                    dve.wait_ge(c_ps, i + 1)
                    v.tensor_scalar(flag[:], psC[:, 0:1], CAP - 0.5, None, ALU.is_gt).then_inc(t_step, 1)
                    dve.wait_ge(t_step, 3 * i + 2)
                    hold(A, dve)
                    v.copy_predicated(thr[:], flag[:], cand[:]).then_inc(t_step, 1)
                    dve.wait_ge(t_step, 3 * i + 3)
            v.tensor_copy(thrf[:], thr[:].bitcast(f32)).then_inc(thr_sb, 1)
            dve.wait_ge(row_ps, 1)
            link(v.tensor_copy(thrrow[:, 0, :], psC[:, 8:16]))
            v.tensor_tensor(gt[:], pb[:], thrrow[:].broadcast_to(full), ALU.is_gt)
            v.tensor_tensor(eq[:], pb[:], thrrow[:].broadcast_to(full), ALU.is_equal).then_inc(mask_sb, 1)
            dve.wait_ge(mask_sb, 1)
            dve.wait_ge(ranked, 2)
            rank_eq = psE[:, 0:(NT + 1) * E8].rearrange("p (t e) -> p t e", e=E8)
            rank_gt = psG[:, 0:(NT + 1) * E8].rearrange("p (t e) -> p t e", e=E8)
            v.tensor_copy(eqr[:], rank_eq[:, 0:NT, :])
            link(v.tensor_scalar(need[:], rank_gt[:, NT:NT + 1, :], -1.0, float(CAP), ALU.mult, ALU.add))
            nb = need[:].broadcast_to(full)
            link(v.tensor_tensor(okk[:], eqr[:], nb, ALU.is_lt))
            link(v.tensor_tensor(okk[:], okk[:], eq[:], ALU.mult))
            v.tensor_tensor(sel[:], okk[:], gt[:], ALU.add)
            link(v.tensor_tensor(eqr[:], eqr[:], nb, ALU.min))
            link(v.tensor_tensor(pos[:], eqr[:], rank_gt[:, 0:NT, :], ALU.add))
            link(v.scalar_tensor_tensor(pos[:], pos[:], 1.0, sel[:], ALU.add, ALU.mult))
            link(v.tensor_scalar(pos[:], pos[:], 1.0, None, ALU.subtract))
            link(v.tensor_copy(posi[:], pos[:]))
            link(v.tensor_scalar(posi[:], posi[:], 7, None, ALU.arith_shift_right))
            link(v.tensor_copy(posh[:], posi[:]))
            v.scalar_tensor_tensor(lo[:], posh[:], -128.0, pos[:], ALU.mult, ALU.add)
            dve.wait_ge(iotas, 1)
            link(v.tensor_tensor(hot4[:], it4[:], posh[:].rearrange("p t e -> p (t e)").unsqueeze(2)
                                 .broadcast_to([128, NT * E8, 4]), ALU.is_equal))
            h4 = hot4[:].rearrange("p (t e) a -> p t e a", e=E8)
            v.tensor_scalar(val[:, :, :, 0, :], h4, tokp[:], None, ALU.mult)
            v.tensor_tensor(val[:, :, :, 1, :], h4, tokt[:].rearrange("p t (e a) -> p t e a", a=4), ALU.mult
                            ).then_inc(val_sb, 1)
            dve.wait_ge(val_sb, 1)

            def hots(e, first):
                for t in range(NT):
                    if t % GRP == 0 and (not first or t >= NHOT):
                        dve.wait_ge(hot_used, (NT // GRP) * e + (t - NHOT) // GRP + 1)
                    last = v.tensor_scalar(hot[:, t % NHOT, :], lane[:], lo[:, t, bass.ds(e, 1)], None, ALU.is_equal)
                    if t % GRP == GRP - 1:
                        last.then_inc(hot_sb, 1)
            hots(0, True)
            with dve.Fori(1, E8) as e:
                hots(e, False)
            dve.wait_ge(hot_used, NT // GRP * E8)
            i4 = psI[:, 0:8 * E8].rearrange("p (e c a) -> p e c a", c=2, a=4)
            link(v.tensor_scalar(idf[:], i4[:, :, 1, :], 128.0, None, ALU.mult))
            v.tensor_tensor(ids[:].rearrange("p (e a) -> p e a", a=4), idf[:], i4[:, :, 0, :], ALU.add)


def experts1(nc, A, tab, acc, ids, fc1T, b1c, fc2T, b2r, lnw, lnb):
    ctx = ExitStack()
    R = D + E8
    C = CAP // 128
    with ctx:
        def sb(name, shape, dt=f32):
            return ctx.enter_context(nc.sbuf_tensor("e1_" + name, shape, dt))

        def sem(name):
            return ctx.enter_context(nc.semaphore("e1_" + name))

        def psum(name):
            return ctx.enter_context(nc.psum_tensor("e1_" + name, [128, 512], f32))
        lw, lb = sb("lw", [D, 1]), sb("lb", [D, 1])
        w1 = [sb(f"w1{p}", [D, F1]) for p in range(2)]
        w2 = [sb(f"w2{p}", [128, 4, D]) for p in range(2)]
        b1 = [sb(f"b1{p}", [128, 4]) for p in range(2)]
        b2 = [sb(f"b2{p}", [1, D]) for p in range(2)]
        ixg = [sb(f"ixg{p}", [128, C], i32) for p in range(2)]
        ixa = [sb(f"ixa{p}", [128, C], i32) for p in range(2)]
        xg = [sb(f"xg{p}", [128, C, R]) for p in range(2)]
        gate = sb("gate", [128, E8 * C])
        st, mv = sb("st", [128, C, 6]), sb("mv", [128, C, 2])
        ve, rs = sb("ve", [128, C, 1]), sb("rs", [128, C, 1])
        yn = [sb(f"yn{p}", [128, C, D]) for p in range(2)]
        yT = [sb(f"yT{p}", [D, CAP]) for p in range(2)]
        hT = [sb(f"hT{p}", [128, 4, CAP]) for p in range(2)]
        ot = [sb(f"ot{p}", [128, C, D]) for p in range(2)]
        psX, psH, psY = psum("psX"), [psum(f"psH{c}") for c in range(4)], [psum(f"psY{p}") for p in range(2)]
        c_in = sem("c_in")
        w_in = [sem(f"w_in{p}") for p in range(2)]
        x_in = [sem(f"x_in{p}") for p in range(2)]
        added = [sem(f"added{p}") for p in range(2)]
        ixg_sb, ixa_sb, step, var, rstd, yn_sb, x_ps, yT_sb, h_ps, h_sb, y_ps, o_sb = (
            sem(n) for n in "ixg_sb ixa_sb step var rstd yn_sb x_ps yT_sb h_ps h_sb y_ps o_sb".split())
        block = ctx.enter_context(nc.Block())

        def iterations(eng, body, last=True):
            body(None, Seq(0, 0))
            body(Seq(0, 0), Seq(0, 1))
            body(Seq(0, 1), Seq(0, 2))
            with eng.Fori(1, E8 // 2 - 1) as j:
                for k in range(2):
                    body(Seq(j, k), Seq(j, k + 1))
            body(Seq(0, E8 - 2), Seq(0, E8 - 1))
            body(Seq(0, E8 - 1), None)

        @block.sync
        def _(sp):
            sp.dma_start(lw[:], lnw).then_inc(c_in, 16)
            sp.dma_start(lb[:], lnb).then_inc(c_in, 16)

            def body(s, n):
                if n:
                    if later(n):
                        sp.wait_ge(y_ps, n.n - 1)
                    for dst, src in ((w1, fc1T), (w2, fc2T), (b1, b1c), (b2, b2r)):
                        sp.dma_start(dst[n.p][:], src[n.n]).then_inc(w_in[n.p], 16)
            iterations(sp, body)

        @block.gpsimd
        def _(pool):
            def gather(m):
                if later(m):
                    pool.wait_ge(yn_sb, m.n - 1)
                    pool.wait_ge(x_in[m.p], 16 * C * m.half)
                nc.gpsimd.tensor_copy(ixg[m.p][:], ids[:, bass.ds(C * m.n, C)]).then_inc(ixg_sb, 1)
                pool.wait_ge(ixg_sb, m.n + 1)
                hold(A, pool)
                for a in range(C):
                    pool.indirect_dma_start(xg[m.p][:, a, :], None, tab,
                                            bass.IndirectOffsetOnAxis(ap=ixg[m.p][:, a:a + 1], axis=0)
                                            ).then_inc(x_in[m.p], 16)

            def body(s, n, g):
                if n:
                    pool.wait_ge(var, n.n + 1)
                    nc.gpsimd.tensor_tensor(rs[:], ve[:], A["mhalf"][:, 0:C], ALU.pow).then_inc(rstd, 1)
                if g:
                    gather(g)
                if s:
                    if later(s):
                        pool.wait_ge(added[s.p], 16 * C * s.half)
                    nc.gpsimd.tensor_copy(ixa[s.p][:], ids[:, bass.ds(C * s.n, C)]).then_inc(ixa_sb, 1)
                    pool.wait_ge(ixa_sb, s.n + 1)
                    pool.wait_ge(o_sb, s.n + 1)
                    if later(s, 1):
                        before = Seq(0, s.n - 1)
                        pool.wait_ge(added[before.p], 16 * C * (before.half + 1))
                    hold(A, pool)
                    for a in range(C):
                        pool.indirect_dma_start(acc, bass.IndirectOffsetOnAxis(ap=ixa[s.p][:, a:a + 1], axis=0),
                                                ot[s.p][:, a, :], None, compute_op=ALU.add).then_inc(added[s.p], 16)
            for i in range(-3, E8):
                body(*(Seq(0, i + ahead) if 0 <= i + ahead < E8 else None for ahead in (0, 2, 3)))
            for p in range(2):
                pool.wait_ge(added[p], 16 * C * (E8 // 2))

        @block.vector
        def _(dve):
            v = nc.vector

            def body(s, n):
                if n:
                    dve.wait_ge(x_in[n.p], 16 * C * (n.half + 1))
                    if later(n, 1):
                        dve.wait_ge(yn_sb, n.n)
                    stp = Steps(dve, step, n, 2)
                    for a in range(C):
                        ins = v.bn_stats(st[:, a, :], xg[n.p][:, a, 0:D])
                    stp(ins)
                    hold(A, dve)
                    for a in range(C):
                        ins = v.bn_aggr(mv[:, a, :], st[:, a, :])
                    stp(ins)
                    v.tensor_scalar(ve[:], mv[:, :, 1:2], EPS, None, ALU.add).then_inc(var, 1)
                    dve.wait_ge(rstd, n.n + 1)
                    if later(n):
                        dve.wait_ge(x_ps, n.n - 1)
                    v.tensor_copy(gate[:, bass.ds(C * n.n, C)], xg[n.p][:, :, bass.ds(n.n + D, 1)].rearrange("p a o -> p (a o)"))
                    for a in range(C):
                        ins = v.tensor_scalar(yn[n.p][:, a, :], xg[n.p][:, a, 0:D], mv[:, a, 0:1], rs[:, a, :],
                                              ALU.subtract, ALU.mult)
                    ins.then_inc(yn_sb, 1)
                if s:
                    dve.wait_ge(y_ps, s.n + 1)
                    if later(s):
                        dve.wait_ge(added[s.p], 16 * C * s.half)
                    for a in range(C):
                        ins = v.tensor_scalar(ot[s.p][:, a, :], psY[s.p][:, D * a:D * a + D],
                                              gate[:, bass.ds(C * s.n + a, 1)], None, ALU.mult)
                    ins.then_inc(o_sb, 1)
            for i in range(-2, 2):
                body(Seq(0, i) if i >= 0 else None, Seq(0, i + 2))
            with dve.Fori(1, E8 // 2 - 1) as j:
                for k in range(2):
                    body(Seq(j, k), Seq(j, k + 2))
            for i in (E8 - 2, E8 - 1):
                body(Seq(0, i), None)

        @block.scalar
        def _(act):
            a_ = nc.scalar
            act.wait_ge(c_in, 32)

            def body(s, n):
                if s:
                    for c in range(4):
                        act.wait_ge(h_ps, 4 * s.n + c + 1)
                        if c == 0:
                            act.wait_ge(w_in[s.p], 64 * (s.half + 1))
                            if later(s):
                                act.wait_ge(y_ps, s.n - 1)
                        a_.activation(hT[s.p][:, c, :], psH[c][:], ACT.Gelu_apprx_tanh, bias=b1[s.p][:, c:c + 1]
                                      ).then_inc(h_sb, 1)
                if n:
                    act.wait_ge(x_ps, n.n + 1)
                    if later(n):
                        act.wait_ge(h_ps, 4 * n.n - 4)
                    a_.activation(yT[n.p][:], psX[:], ACT.Identity, bias=lb[:], scale=lw[:]).then_inc(yT_sb, 1)
            iterations(act, body)

        @block.tensor
        def _(pe):
            mm = nc.tensor.matmul

            def body(s, n):
                if s:
                    pe.wait_ge(yT_sb, s.n + 1)
                    pe.wait_ge(w_in[s.p], 64 * (s.half + 1))
                    for c in range(4):
                        if later(s, 1):
                            pe.wait_ge(h_sb, 4 * s.n + c - 3)
                        mm(psH[c][:], w1[s.p][:, 128 * c:128 * c + 128], yT[s.p][:], start=True, stop=True
                           ).then_inc(h_ps, 1)
                if n:
                    pe.wait_ge(yn_sb, n.n + 1)
                    if later(n, 1):
                        pe.wait_ge(yT_sb, n.n)
                    for a in range(C):
                        last = nc.tensor.transpose(psX[:, 128 * a:128 * a + 128], yn[n.p][:, a, :], A["ident"][:])
                    last.then_inc(x_ps, 1)
                if s:
                    pe.wait_ge(h_sb, 4 * s.n + 4)
                    if later(s):
                        pe.wait_ge(o_sb, s.n - 1)
                    for a in range(C):
                        o = psY[s.p][:, D * a:D * a + D]
                        for c in range(4):
                            mm(o, hT[s.p][:, c, 128 * a:128 * a + 128], w2[s.p][:, c, :], start=(c == 0), stop=False)
                        last = mm(o, A["ones"][0:1, :], b2[s.p][:], start=False, stop=True, tile_position=(0, 0))
                    last.then_inc(y_ps, 1)
            iterations(pe, body)


def finish(nc, A, acc, out):
    ctx = ExitStack()
    G = 4
    NG = NT // G
    with ctx:
        def sb(name, shape, dt=f32):
            return ctx.enter_context(nc.sbuf_tensor("fn_" + name, shape, dt))

        def sem(name):
            return ctx.enter_context(nc.semaphore("fn_" + name))
        x = [sb(f"x{p}", [128, G, D]) for p in range(2)]
        o = [sb(f"o{p}", [128, G, D]) for p in range(2)]
        st, mv, ve, rs = sb("st", [128, G, 6]), sb("mv", [128, G, 2]), sb("ve", [128, G, 1]), sb("rs", [128, G, 1])
        x_in = [sem(f"x_in{p}") for p in range(2)]
        stored = [sem(f"stored{p}") for p in range(2)]
        step, var, rstd, o_sb = (sem(n) for n in "step var rstd o_sb".split())
        block = ctx.enter_context(nc.Block())
        av = acc.rearrange("(g t p) d -> g p t d", t=G, p=128)
        ov = out.rearrange("(g t p) d -> g p t d", t=G, p=128)

        def groups(eng, body):
            for k in range(2):
                body(Seq(0, k))
            with eng.Fori(1, NG // 2) as j:
                for k in range(2):
                    body(Seq(j, k))

        @block.sync
        def _(sp):
            def load(s):
                if later(s):
                    sp.wait_ge(o_sb, s.n - 1)
                sp.dma_start(x[s.p][:], av[s.n]).then_inc(x_in[s.p], 16)
            groups(sp, load)

        @block.gpsimd
        def _(pool):
            def body(s):
                pool.wait_ge(var, s.n + 1)
                nc.gpsimd.tensor_tensor(rs[:], ve[:], A["mhalf"][:, 0:G], ALU.pow).then_inc(rstd, 1)
            groups(pool, body)

        @block.scalar
        def _(act):
            def store(s):
                act.wait_ge(o_sb, s.n + 1)
                act.dma_start(ov[s.n], o[s.p][:]).then_inc(stored[s.p], 16)
            groups(act, store)
            for p in range(2):
                act.wait_ge(stored[p], 16 * (NG // 2))

        @block.vector
        def _(dve):
            v = nc.vector

            def body(s):
                dve.wait_ge(x_in[s.p], 16 * (s.half + 1))
                stp = Steps(dve, step, s, 2)
                for a in range(G):
                    ins = v.bn_stats(st[:, a, :], x[s.p][:, a, :])
                stp(ins)
                hold(A, dve)
                for a in range(G):
                    ins = v.bn_aggr(mv[:, a, :], st[:, a, :])
                stp(ins)
                v.tensor_scalar(ve[:], mv[:, :, 1:2], EPS, None, ALU.add).then_inc(var, 1)
                dve.wait_ge(rstd, s.n + 1)
                if later(s):
                    dve.wait_ge(stored[s.p], 16 * s.half)
                for a in range(G):
                    ins = v.tensor_scalar(o[s.p][:, a, :], x[s.p][:, a, :], mv[:, a, 0:1], rs[:, a, :],
                                          ALU.subtract, ALU.mult)
                ins.then_inc(o_sb, 1)
            groups(dve, body)


def build(nc, x, qkv0, wo0, router, fc, pj, qkv1, b1col, b1row, off, lin2, lin2b, gate, lnw, lnb, fc1, b1s, fc2, b2s, out):
    ctx = ExitStack()
    with ctx:
        def sb(name, shape, dt=f32):
            return ctx.enter_context(nc.sbuf_tensor(name, shape, dt))

        def sem(name):
            return ctx.enter_context(nc.semaphore(name))

        def dram(name, shape, dt=f32):
            return nc.dram_tensor(name, shape, dt).ap()
        A = {"ident": sb("ident", [128, 128]), "identb": sb("identb", [128, 128], bf16),
             "mhalf": sb("mhalf", [128, 8, 1]), "ones": sb("ones", [128, 128]),
             "onesb": sb("onesb", [128, 128], bf16), "below": sb("below", [128, 128], bf16),
             "held": sem("held")}
        zero = sb("zero", [128, D])
        fcs, pjs = sb("fcs", [D, E8, F0]), sb("pjs", [128, E8, 4, D])
        logits = sb("logits", [128, NT, E8])
        slot, tile_expert = sb("slot", [128, NT], i32), sb("tile_expert", [128, NS], i32)
        ids = sb("ids", [128, E8 * (CAP // 128)], i32)
        x1d = dram("x1d", [NTOK, D])
        qkd = [dram(f"qkd{p}", [2, 3, D, T], bf16) for p in range(2)]
        xs, ys = dram("xs", [NS * 128, D]), dram("ys", [NS * 128, D])
        tab, acc = dram("tab", [NTOK, D + E8]), dram("acc", [NTOK, D])
        filled, early = sem("filled"), sem("early")
        with nc.Block() as block:
            @block.gpsimd
            def _(pool):
                g = nc.gpsimd
                for name, value in (("ident", 0.0), ("identb", 0.0), ("mhalf", -0.5), ("ones", 1.0), ("onesb", 1.0),
                                    ("below", 1.0)):
                    g.memset(A[name][:], value)
                g.memset(zero[:], 0.0).then_inc(filled, 1)
                pool.wait_ge(filled, 1)
                for m in (A["ident"], A["identb"]):
                    g.affine_select(out=m[:], in_=m[:], pattern=[[-1, 128]], compare_op=ALU.not_equal, fill=1.0,
                                    base=0, channel_multiplier=1)
                g.affine_select(out=A["below"][:], in_=A["below"][:], pattern=[[1, 128]], compare_op=ALU.is_gt,
                                fill=0.0, base=0, channel_multiplier=-1).then_inc(filled, 1)
                pool.wait_ge(filled, 2)

            @block.sync
            def _(sp):
                sp.wait_ge(filled, 1)
                sp.dma_start(xs.rearrange("(s p) d -> p s d", p=128),
                             zero[:].unsqueeze(1).broadcast_to([128, NS, D])).then_inc(early, 16)
                sp.dma_start(fcs[:], fc).then_inc(early, 16)
                sp.dma_start(pjs[:], pj).then_inc(early, 16)
        attention0(nc, A, x, x1d, qkd, qkv0, wo0, router, logits)
        route0(nc, A, x1d, xs, logits, slot, tile_expert, early)
        experts0(nc, A, xs, ys, fcs, pjs, tile_expert)
        attention1(nc, A, x1d, ys, slot, qkv1, b1col, b1row, off, lin2, lin2b, gate, tab[:, 0:D], acc, logits)
        choose1(nc, A, logits, tab[:, D:D + E8], ids)
        experts1(nc, A, tab, acc, ids, fc1, b1s, fc2, b2s, lnw, lnb)
        finish(nc, A, acc, out)


def kernel(**inputs):
    import numpy as np
    import concourse.bacc as bacc
    from concourse.bass_utils import run_bass_kernel_spmd

    def a(name):
        return np.asarray(inputs[name])

    w0 = a("L0_attn_in_proj_weight").T

    def by_dim(w):
        return w.reshape(D, H0, DH0).transpose(0, 2, 1).reshape(D, D)

    arrays = {
        "x": a("L0_attn_query").reshape(NTOK, D),
        "qkv0": np.concatenate([by_dim(w0[:, 0:D]), by_dim(w0[:, D:2 * D]), w0[:, 2 * D:]], axis=1),
        "wo0": a("L0_attn_out_proj_weight").T,
        "router": a("L0_ffn_router_w").T,
        "fc": a("L0_ffn_expert_fc").transpose(1, 0, 2),
        "pj": a("L0_ffn_expert_proj").transpose(2, 0, 1).reshape(4, 128, E8, D).transpose(1, 2, 0, 3),
        "qkv1": a("L1_attn_qkv_w").T,
        "b1col": a("L1_attn_qkv_b").reshape(3, D).T,
        "b1row": a("L1_attn_qkv_b")[None, 2 * D:],
        "off": a("L1_attn_off_w").T,
        "lin2": a("L1_attn_lin2_w").T,
        "lin2b": a("L1_attn_lin2_b")[None, :],
        "gate": a("L1_ffn_gate_w").T,
        "lnw": a("L1_ffn_ln_w")[:, None],
        "lnb": a("L1_ffn_ln_b")[:, None],
        "fc1": a("L1_ffn_fc1s").transpose(0, 2, 1),
        "b1s": a("L1_ffn_b1s").reshape(E8, 4, 128).transpose(0, 2, 1),
        "fc2": a("L1_ffn_fc2s").transpose(0, 2, 1).reshape(E8, 4, 128, D).transpose(0, 2, 1, 3),
        "b2s": a("L1_ffn_b2s")[:, None, :],
    }
    arrays = {f"in_{n}": np.ascontiguousarray(v) for n, v in arrays.items()}
    nc = bacc.Bacc("TRN2", target_bir_lowering=False, num_devices=1)
    args = [nc.dram_tensor(n, v.shape, mybir.dt.from_np(v.dtype), kind="ExternalInput").ap() for n, v in arrays.items()]
    out = nc.dram_tensor("out_x", (NTOK, D), f32, kind="ExternalOutput").ap()
    build(nc, *args, out)
    r = run_bass_kernel_spmd(nc, [arrays], core_ids=[0])
    return np.asarray(r.results[0]["out_x"]).reshape(NB, T, D)
```
